# Optimizing a Trainium2 kernel written in Bass

```python
import numpy as np
import jax
import jax.numpy as jnp

def _softmax(x, axis=-1):
    return jax.nn.softmax(x, axis=axis)
def _gelu(x):
    return jax.nn.gelu(x, approximate=True)
def _silu(x):
    return jax.nn.silu(x)
def _sigmoid(x):
    return jax.nn.sigmoid(x)
def _layernorm(x, axis=-1, eps=1e-5):
    m = jnp.mean(x, axis=axis, keepdims=True)
    v = jnp.var(x, axis=axis, keepdims=True)
    return (x - m) / jnp.sqrt(v + eps)
def _scatter_add(tgt, idx, src, axis=0):
    return tgt.at[idx].add(src)
def _segment_sum(src, seg, n):
    return jax.ops.segment_sum(src, seg, n)

kernel_name = 'mk_conv_preact_d2_conv_nchw768_32eb48'

def setup_inputs(seed: int = 0):
    np.random.seed(seed)
    _w = jnp.asarray
    def _rec_inputs():
        import jax
        import jax.numpy as jnp
        _gk = jax.random.key(seed)
        x = -0.0001538 + 1 * jax.random.normal(jax.random.fold_in(_gk, 1), (2, 768, 64, 64), jnp.float32)
        return x
    x = _rec_inputs()
    def _L0_conv_setup():
        import jax, jax.numpy as jnp
        import numpy as np
        B, DM, H, W = (2, 768, 64, 64)
        EXPAND, DSTATE, DCONV = (2, 4, 3)
        DI = DM * EXPAND
        R = DM // 16
        key = jax.random.key(seed)
        ks = jax.random.split(key, 8)
        s = 0.02
        dt = jnp.exp(jax.random.uniform(ks[5], (1, DI)) * (np.log(0.1) - np.log(0.001)) + np.log(0.001))
        dt = jnp.clip(dt, 0.0001)
        inv_dt = dt + jnp.log(-jnp.expm1(-dt))
        A_log = jnp.log(jnp.arange(1, DSTATE + 1, dtype=jnp.float32))
        A_log = jnp.broadcast_to(A_log[None, None, :], (1, DI, DSTATE))
        return {'hidden_states': jax.random.normal(ks[0], (B, DM, H, W), jnp.float32), 'in_proj_w': jax.random.normal(ks[1], (DI, DM), jnp.float32) * s, 'conv_w': jax.random.normal(ks[2], (DI, 1, DCONV, DCONV), jnp.float32) * s, 'conv_b': jnp.zeros((DI,), jnp.float32), 'x_proj_w': jax.random.normal(ks[3], (R + 2 * DSTATE, DI), jnp.float32) * s, 'dt_w': jax.random.uniform(ks[4], (1, DI, R), jnp.float32, -R ** (-0.5), R ** (-0.5)), 'dt_b': inv_dt, 'A_log': A_log, 'D_param': jnp.ones((1, DI), jnp.float32), 'ln_g': jnp.ones((DI,), jnp.float32), 'ln_b': jnp.zeros((DI,), jnp.float32), 'out_proj_w': jax.random.normal(ks[6], (DM, DI), jnp.float32) * s}
    _L0_conv_all = _L0_conv_setup()
    _L0_conv_in = {k: v for k, v in _L0_conv_all.items() if k in ('in_proj_w', 'conv_w', 'conv_b', 'x_proj_w', 'dt_w', 'dt_b', 'A_log', 'D_param', 'ln_g', 'ln_b', 'out_proj_w', )}
    del _L0_conv_all

    def _L1_conv_setup():
        import jax, jax.numpy as jnp
        import numpy as np
        HEADS = 12
        key = jax.random.key(seed)
        k1, k2, k3 = jax.random.split(key, 3)
        B, C, H, W = (16, 768, 64, 64)
        x = jax.random.normal(k1, (B, C, H, W), dtype=jnp.float32)
        W_qkv = jax.random.normal(k2, (C, C), dtype=jnp.float32) * 0.02
        W_out = jax.random.normal(k3, (C, C), dtype=jnp.float32) * 0.02
        temp = jnp.ones((HEADS, 1), dtype=jnp.float32)
        return {'x': x, 'W_qkv': W_qkv, 'W_out': W_out, 'temp': temp}
    _L1_conv_all = _L1_conv_setup()
    _L1_conv_in = {k: v for k, v in _L1_conv_all.items() if k in ('W_qkv', 'W_out', 'temp', )}
    del _L1_conv_all

    return {
        "x": x,
        "L0_conv_in_proj_w": _L0_conv_in["in_proj_w"],
        "L0_conv_conv_w": _L0_conv_in["conv_w"],
        "L0_conv_conv_b": _L0_conv_in["conv_b"],
        "L0_conv_x_proj_w": _L0_conv_in["x_proj_w"],
        "L0_conv_dt_w": _L0_conv_in["dt_w"],
        "L0_conv_dt_b": _L0_conv_in["dt_b"],
        "L0_conv_A_log": _L0_conv_in["A_log"],
        "L0_conv_D_param": _L0_conv_in["D_param"],
        "L0_conv_ln_g": _L0_conv_in["ln_g"],
        "L0_conv_ln_b": _L0_conv_in["ln_b"],
        "L0_conv_out_proj_w": _L0_conv_in["out_proj_w"],
        "L1_conv_W_qkv": _L1_conv_in["W_qkv"],
        "L1_conv_W_out": _L1_conv_in["W_out"],
        "L1_conv_temp": _L1_conv_in["temp"],
    }

def reference(x, L0_conv_in_proj_w, L0_conv_conv_w, L0_conv_conv_b, L0_conv_x_proj_w, L0_conv_dt_w, L0_conv_dt_b, L0_conv_A_log, L0_conv_D_param, L0_conv_ln_g, L0_conv_ln_b, L0_conv_out_proj_w, L1_conv_W_qkv, L1_conv_W_out, L1_conv_temp):
    import jax
    import jax.numpy as jnp
    def _L0_conv_ref(hidden_states, in_proj_w, conv_w, conv_b, x_proj_w, dt_w, dt_b, A_log, D_param, ln_g, ln_b, out_proj_w):
        import jax, jax.numpy as jnp
        import numpy as np
        B, DM, H, W = (2, 768, 64, 64)
        EXPAND, DSTATE, DCONV = (2, 4, 3)
        DI = DM * EXPAND
        R = DM // 16
        b, dm, h, w = hidden_states.shape
        L = h * w
        hs = jnp.transpose(hidden_states, (0, 2, 3, 1))
        x = hs @ in_proj_w.T
        xs = jnp.transpose(x, (0, 3, 1, 2))
        pad = (DCONV - 1) // 2
        xs = jax.lax.conv_general_dilated(xs, conv_w, (1, 1), ((pad, pad), (pad, pad)), feature_group_count=xs.shape[1], dimension_numbers=('NCHW', 'OIHW', 'NCHW')) + conv_b[None, :, None, None]
        xs = xs * jax.nn.sigmoid(xs)
        xs_seq = jnp.transpose(xs, (0, 2, 3, 1)).reshape(b, L, -1)
        x_dbl = xs_seq @ x_proj_w.T
        dt, Bs, Cs = jnp.split(x_dbl, [R, R + DSTATE], axis=-1)
        delta = jnp.einsum('blr,dr->bdl', dt, dt_w[0])
        delta = jax.nn.softplus(delta + dt_b[0][None, :, None])
        u = jnp.transpose(xs_seq, (0, 2, 1))
        A = -jnp.exp(A_log[0])
        dA = jnp.exp(delta[..., None] * A[None, :, None, :])
        dBu = (delta * u)[..., None] * Bs[:, None, :, :]

        def comb(e1, e2):
            a1, x1 = e1
            a2, x2 = e2
            return (a2 * a1, a2 * x1 + x2)
        _, states = jax.lax.associative_scan(comb, (dA, dBu), axis=2)
        y = jnp.einsum('bdln,bln->bdl', states, Cs) + D_param[0][None, :, None] * u
        y = jnp.transpose(y, (0, 2, 1))
        mu = y.mean(-1, keepdims=True)
        var = y.var(-1, keepdims=True)
        y = (y - mu) * jax.lax.rsqrt(var + 1e-05) * ln_g + ln_b
        y = y.reshape(b, h, w, -1)
        out = y @ out_proj_w.T
        return jnp.transpose(out, (0, 3, 1, 2))

    def _L1_conv_ref(x, W_qkv, W_out, temp):
        import jax, jax.numpy as jnp
        import numpy as np
        HEADS = 12
        B, C, H, W = x.shape
        N = H * W
        d = C // HEADS
        x3 = jnp.transpose(x, (0, 2, 3, 1)).reshape(B, N, C)
        w = (x3 @ W_qkv.T).reshape(B, N, HEADS, d).transpose(0, 2, 1, 3)
        norm = jnp.sqrt(jnp.sum(w * w, axis=2, keepdims=True))
        w_normed = w / jnp.maximum(norm, 1e-12)
        w_sq = w_normed ** 2
        logits = jnp.sum(w_sq, axis=-1) * temp
        Pi = jax.nn.softmax(logits, axis=1)
        Pi_n = Pi / (jnp.sum(Pi, axis=-1, keepdims=True) + 1e-08)
        dots = jnp.einsum('bhn,bhnd->bhd', Pi_n, w ** 2)[:, :, None, :]
        attn = 1.0 / (1.0 + dots)
        out = -(w * Pi[..., None]) * attn
        out = out.transpose(0, 2, 1, 3).reshape(B, N, C)
        out = out @ W_out.T
        return out.reshape(B, H, W, C).transpose(0, 3, 1, 2)

    def _gn(v, G=32, eps=1e-5):
        B_, C_, H_, W_ = v.shape
        g = v.reshape(B_, G, C_ // G, H_, W_)
        m = jnp.mean(g, axis=(2, 3, 4), keepdims=True)
        s = jnp.var(g, axis=(2, 3, 4), keepdims=True)
        return ((g - m) / jnp.sqrt(s + eps)).reshape(v.shape)

    def _ln_c(v, eps=1e-6):
        m = jnp.mean(v, axis=1, keepdims=True)
        s = jnp.var(v, axis=1, keepdims=True)
        return (v - m) / jnp.sqrt(s + eps)

    def _ln_t(v, eps=1e-5):
        m = jnp.mean(v, axis=-1, keepdims=True)
        s = jnp.var(v, axis=-1, keepdims=True)
        return (v - m) / jnp.sqrt(s + eps)

    def _to_tokens(v):
        B_, C_, H_, W_ = v.shape
        return v.reshape(B_, C_, H_ * W_).transpose(0, 2, 1)
    def _from_tokens(t, like):
        B_, C_, H_, W_ = like.shape
        return t.transpose(0, 2, 1).reshape(B_, C_, H_, W_)

    x = x + _L0_conv_ref(_gn(x), L0_conv_in_proj_w, L0_conv_conv_w, L0_conv_conv_b, L0_conv_x_proj_w, L0_conv_dt_w, L0_conv_dt_b, L0_conv_A_log, L0_conv_D_param, L0_conv_ln_g, L0_conv_ln_b, L0_conv_out_proj_w)
    x = x + _L1_conv_ref(_gn(x), L1_conv_W_qkv, L1_conv_W_out, L1_conv_temp)
    return x


_drawn_inputs = setup_inputs


def setup_inputs(seed=0):
    import zlib

    import numpy as np

    out = dict(_drawn_inputs(seed))
    spreads = {'L0_conv_conv_b': (0.0, 0.1),
     'L0_conv_D_param': (1.0, 0.2),
     'L0_conv_ln_g': (1.0, 0.2),
     'L0_conv_ln_b': (0.0, 0.1),
     'L1_conv_temp': (1.0, 0.6)}
    factors = {'L0_conv_x_proj_w': 8.0,
     'L0_conv_dt_w': 8.0,
     'L0_conv_dt_b': 8.0,
     'L0_conv_A_log': 8.0,
     'L1_conv_W_qkv': 3.797,
     'L1_conv_W_out': 3.797}
    for name, (base, spread) in spreads.items():
        noise = np.random.default_rng([zlib.crc32(name.encode()), seed]).standard_normal(out[name].shape)
        drawn = base * np.exp(spread * noise) if base else spread * noise
        out[name] = jnp.asarray(drawn.astype(out[name].dtype))
    for name, factor in factors.items():
        out[name] = (out[name] * factor).astype(out[name].dtype)
    return out
```

```python
from contextlib import ExitStack

import concourse.bass as bass
from concourse import mybir
from concourse.alu_op_type import AluOpType as ALU

F32 = mybir.dt.float32
ACT = mybir.ActivationFunctionType
AX = mybir.AxisListType

P = 128
EXPSET = "natural_log_exp_and_others"


def wait(eng, sem, value):
    if value > 0:
        eng.wait_ge(sem, value)


def group_norm_scale(vec, pe, act, nc, s, stats, nstat, tmp, psum, quad, eps, scale, bias):
    own, dev, mean_g, var_g = tmp[:, 0:2], tmp[:, 2:3], tmp[:, 3:4], tmp[:, 4:5]
    lg, half = tmp[:, 5:6], tmp[:, 6:7]
    v, p, a = s

    def vector_steps(v0, p0, a0):
        nc.vector.bn_aggr(own, stats.rearrange("p n s -> p (n s)")).then_inc(v, 1)
        vec.wait_ge(p, p0 + 1)
        nc.vector.tensor_copy(mean_g, psum[:, 0:1]).then_inc(v, 1)
        vec.wait_ge(v, v0 + 2)
        nc.vector.tensor_sub(dev, own[:, 0:1], mean_g).then_inc(v, 1)
        vec.wait_ge(v, v0 + 3)
        nc.vector.tensor_mul(dev, dev, dev).then_inc(v, 1)
        vec.wait_ge(v, v0 + 4)
        nc.vector.tensor_add(dev, dev, own[:, 1:2]).then_inc(v, 1)
        vec.wait_ge(p, p0 + 2)
        nc.vector.tensor_scalar(var_g, psum[:, 1:2], eps, None, ALU.add).then_inc(v, 1)
        vec.wait_ge(a, a0 + 2)
        nc.vector.tensor_mul(lg, half, half).then_inc(v, 1)
        vec.wait_ge(v, v0 + 7)
        nc.vector.tensor_mul(lg, lg, var_g).then_inc(v, 1)
        vec.wait_ge(v, v0 + 8)
        nc.vector.tensor_scalar(lg, lg, -0.5, 1.5, ALU.mult, ALU.add).then_inc(v, 1)
        vec.wait_ge(v, v0 + 9)
        nc.vector.tensor_mul(scale, lg, half).then_inc(v, 1)
        vec.wait_ge(v, v0 + 10)
        nc.vector.tensor_scalar(bias, mean_g, scale, -1.0, ALU.mult, ALU.mult).then_inc(v, 1)

    def tensor_steps(v0, p0, a0):
        pe.wait_ge(v, v0 + 1)
        nc.tensor.matmul(psum[:, 0:1], quad, own[:, 0:1], start=True, stop=True).then_inc(p, 1)
        pe.wait_ge(v, v0 + 5)
        nc.tensor.matmul(psum[:, 1:2], quad, dev, start=True, stop=True).then_inc(p, 1)

    def scalar_steps(v0, p0, a0):
        act.wait_ge(v, v0 + 6)
        nc.scalar.activation(lg, var_g, ACT.Ln).then_inc(a, 1)
        act.wait_ge(a, a0 + 1)
        nc.scalar.activation(half, lg, ACT.Exp, scale=-0.5).then_inc(a, 1)

    return vector_steps, tensor_steps, scalar_steps


GN_V, GN_P, GN_A = 11, 2, 2


def build(nc, x, win, wout, xpw, dtw, cw, cols, alog, wqkv, wo2, temp, quad_d, pick_d, sel_d, selb_d,
          ident_d, out):
    B, C, H, W = x.shape
    T = H * W
    ROWS = 8
    N = ROWS * W
    CPB = H // ROWS
    NCH = B * CPB
    XT = C // P
    K = win.shape[0]
    NT = NCH * K
    R = dtw.shape[0]
    NS = 4
    PW = W + 2
    XTR = x.rearrange("b (p t) h w -> b p t (h w)", t=XT)
    OUTR = out.rearrange("b (p t) h w -> b p t (h w)", t=XT)

    x1_d = nc.dram_tensor("x1_scratch", [B, P, XT, T], F32).ap()
    woc_d = nc.dram_tensor("wout_scratch", [XT, P, K, P], F32).ap()
    bc_d = nc.dram_tensor("bc_scratch", [NCH, 2 * NS, N], F32).ap()

    with ExitStack() as keep:
        def sbk(name, shape):
            return keep.enter_context(nc.sbuf_tensor(name, shape, F32))

        quad = sbk("quad", [P, P])
        gsc = sbk("gsc", [P, 2 * B])
        gbi = sbk("gbi", [P, 2 * B])
        stats1 = sbk("stats1", [P, B, CPB * XT, 6])
        gtmp = sbk("gtmp", [P, 8])

        shared = dict(B=B, C=C, T=T, N=N, ROWS=ROWS, W=W, CPB=CPB, NCH=NCH, XT=XT, K=K, NT=NT, R=R, NS=NS, PW=PW,
                      XTR=XTR, OUTR=OUTR, x1_d=x1_d, woc_d=woc_d, bc_d=bc_d, quad=quad, gsc=gsc, gbi=gbi,
                      stats1=stats1, gtmp=gtmp, win=win, wout=wout, xpw=xpw, dtw=dtw, cw=cw, cols=cols,
                      alog=alog, wqkv=wqkv, wo2=wo2, temp=temp, quad_d=quad_d, pick_d=pick_d, sel_d=sel_d,
                      selb_d=selb_d, ident_d=ident_d)
        layer0(nc, shared)
        layer1(nc, shared)


def layer0(nc, g):
    (B, C, T, N, ROWS, W, CPB, NCH, XT, K, NT, R, NS, PW) = (
        g[n] for n in "B C T N ROWS W CPB NCH XT K NT R NS PW".split())
    XTR, x1_d, woc_d, bc_d = g["XTR"], g["x1_d"], g["woc_d"], g["bc_d"]
    quad, gsc, gbi, stats1, gtmp = g["quad"], g["gsc"], g["gbi"], g["stats1"], g["gtmp"]
    DI = K * P
    with ExitStack() as ctx:
        def sb(name, shape):
            return ctx.enter_context(nc.sbuf_tensor(name, shape, F32))

        cwt = sb("conv_w", [P, K, 9])
        colt = sb("cols", [P, 5, K])
        At = sb("A", [P, K * NS])
        xpt = sb("xproj_w", [P, K, R + 2 * NS])
        dtt = sb("dt_w", [R, DI])
        bm = sb("b_m", [P, XT])
        pick = sb("pick", [P, 2, P])
        ones32 = sb("ones32", [P, 32])
        convb, dtb, Dp, lng, lnb = (colt[:, n, :] for n in range(5))

        with ExitStack() as c0:
            NXR = 4
            xs = c0.enter_context(nc.sbuf_tensor("xstage", [P, NXR, T], F32))
            stats0 = c0.enter_context(nc.sbuf_tensor("stats0", [P, B, CPB * XT, 6], F32))
            wst = c0.enter_context(nc.sbuf_tensor("wstage", [P, K, C], F32))
            wsg = c0.enter_context(nc.sbuf_tensor("wscaled", [P, K, C], F32))
            avg = c0.enter_context(nc.sbuf_tensor("avg", [P, P], F32))
            pm = c0.enter_context(nc.psum_tensor("pm", [P, 2, 512], F32))
            pb = c0.enter_context(nc.psum_tensor("pb", [P, 512], F32))
            pg = c0.enter_context(nc.psum_tensor("pg", [P, 512], F32))
            s_par = c0.enter_context(nc.semaphore("s_par"))
            s_wst = c0.enter_context(nc.semaphore("s_wst"))
            s_xs = [c0.enter_context(nc.semaphore(f"s_xs{n}")) for n in range(NXR)]
            s_st = c0.enter_context(nc.semaphore("s_st"))
            s_gv = c0.enter_context(nc.semaphore("s_gv"))
            s_gp = c0.enter_context(nc.semaphore("s_gp"))
            s_ga = c0.enter_context(nc.semaphore("s_ga"))
            s_set = c0.enter_context(nc.semaphore("s_set"))
            s_wsg = c0.enter_context(nc.semaphore("s_wsg"))
            s_cm = c0.enter_context(nc.semaphore("s_colmean"))
            s_bmp = c0.enter_context(nc.semaphore("s_bmp"))
            s_cen = c0.enter_context(nc.semaphore("s_cen"))
            s_wod = c0.enter_context(nc.semaphore("s_wod"))
            s_A = c0.enter_context(nc.semaphore("s_A"))
            H2 = C // 2
            params = [(cwt[:], g["cw"]), (colt[:], g["cols"]), (At[:], g["alog"]), (xpt[:], g["xpw"]),
                      (dtt[:], g["dtw"]), (quad[:], g["quad_d"]), (pick[:], g["pick_d"])]
            NB = T // 512
            with nc.Block() as block:
                @block.sync
                def _(sp):
                    for dst, src in params:
                        sp.dma_start(dst, src).then_inc(s_par, 16)
                    for n in range(B * XT):
                        b, t = divmod(n, XT)
                        wait(sp, s_st, NB * (n - NXR + 1))
                        sp.dma_start(xs[:, n % NXR, :], XTR[b, :, t, :]).then_inc(s_xs[n % NXR], 16)
                        if n == 3:
                            sp.dma_start(wst[:], g["wout"]).then_inc(s_wst, 16)
                    sp.wait_ge(s_cen, 2 * K)
                    for m in range(XT):
                        sp.dma_start(woc_d[m], wsg[:, :, m * P:(m + 1) * P]).then_inc(s_wod, 16)
                    sp.wait_ge(s_wod, 16 * XT)

                def steps(b):
                    return group_norm_scale(nc.vector, nc.tensor, nc.scalar, nc, (s_gv, s_gp, s_ga),
                                            stats0[:, b], NB * XT, gtmp, pg, quad[:], 1e-5,
                                            gsc[:, b:b + 1], gbi[:, b:b + 1])

                @block.vector
                def _(vec):
                    nc.vector.memset(avg[:], 1.0 / DI).then_inc(s_set, 1)
                    nc.vector.memset(ones32[:], 1.0).then_inc(s_set, 1)
                    for n in range(B * XT):
                        b, t = divmod(n, XT)
                        vec.wait_ge(s_xs[n % NXR], 16 * (n // NXR + 1))
                        for q in range(NB):
                            nc.vector.bn_stats(stats0[:, b, t * NB + q, :],
                                               xs[:, n % NXR, q * 512:(q + 1) * 512]).then_inc(s_st, 1)
                    vec.wait_ge(s_par, 16 * len(params))
                    vec.wait_ge(s_st, NB * B * XT)
                    for b in range(B):
                        v0, p0, a0 = b * GN_V, b * GN_P, b * GN_A
                        wait(vec, s_gv, v0)
                        steps(b)[0](v0, p0, a0)
                    vec.wait_ge(s_cm, 2)
                    vec.wait_ge(s_wsg, K)
                    for k in range(K):
                        for h in range(2):
                            o = wsg[:, k, h * H2:(h + 1) * H2]
                            nc.vector.tensor_sub(o, o, pm[:, h, 0:H2]).then_inc(s_cen, 1)
                    vec.wait_ge(s_bmp, 1)
                    nc.vector.tensor_copy(bm[:], pb[:, 0:XT]).then_inc(s_set, 1)

                @block.scalar
                def _(act):
                    nc.scalar.preload_act_table_set(EXPSET)
                    act.wait_ge(s_par, 16 * len(params))
                    nc.scalar.activation(At[:], At[:], ACT.Exp).then_inc(s_A, 1)
                    act.wait_ge(s_A, 1)
                    nc.scalar.mul(At[:], At[:], -1.0).then_inc(s_A, 1)
                    act.wait_ge(s_wst, 16)
                    for k in range(K):
                        nc.scalar.activation(wsg[:, k, :], wst[:, k, :], ACT.Copy,
                                             scale=lng[:, k:k + 1]).then_inc(s_wsg, 1)
                    for b in range(B):
                        steps(b)[2](b * GN_V, b * GN_P, b * GN_A)

                @block.tensor
                def _(pe):
                    pe.wait_ge(s_set, 1)
                    pe.wait_ge(s_wsg, K)
                    for h in range(2):
                        for k in range(K):
                            last = nc.tensor.matmul(pm[:, h, 0:H2], avg[:], wsg[:, k, h * H2:(h + 1) * H2],
                                                    start=(k == 0), stop=(k == K - 1))
                        last.then_inc(s_cm, 1)
                    for m in range(XT):
                        for k in range(K):
                            last = nc.tensor.matmul(pb[:, m:m + 1], wst[:, k, m * P:(m + 1) * P],
                                                    lnb[:, k:k + 1], start=(k == 0), stop=(k == K - 1))
                    last.then_inc(s_bmp, 1)
                    for b in range(B):
                        steps(b)[1](b * GN_V, b * GN_P, b * GN_A)

        NW, NV, NX, NU, NG = 3, 3, 3, 3, 3
        HALF = K // 2
        WR = sb("win_ring", [P, NW, XT, P])
        OR = sb("wout_ring", [P, 3, HALF, P])
        VS = sb("v_slots", [P, NV, ROWS + 2, PW])
        HA = sb("halo", [P, K, 2, W])
        UY = sb("uy", [P, NU, K, N])
        BB = sb("B_bc", [P, 2, NS, N])
        CB = sb("C_bc", [P, NS, N])
        XN = sb("xn", [P, XT, N + W])
        XR = sb("x_res", [P, NX, N])
        TO = sb("t_out", [P, N])
        G = sb("g_ring", [P, NG, NS, N])
        EE = sb("sp_e", [P, N])
        LL = sb("sp_l", [P, N])
        RR = sb("sp_r", [P, 2, N])
        TM = sb("sp_t", [P, N])
        SQ = sb("sq", [P, N])
        LS = sb("ln_sums", [P, N])
        MS = sb("ln_msq", [P, N])
        RS = sb("ln_rstd", [P, N])
        XD = sb("x_dbl", [R + 2 * NS, N])
        ST = sb("state", [P, K, NS])

        def ps(name, shape):
            return ctx.enter_context(nc.psum_tensor(name, shape, F32))

        p_in, p_cv, p_dt, p_ln, p_ms = (ps(n, [P, N]) for n in ("p_in", "p_cv", "p_dt", "p_ln", "p_ms"))
        NDA = 3
        p_da = ps("p_da", [P, NDA, N])

        def sem(name):
            return ctx.enter_context(nc.semaphore(name))

        s_win = [sem(f"s_win{n}") for n in range(NW)]
        s_wor = [sem(f"s_wor{n}") for n in range(3)]
        s_xin, s_bw, s_b, s_c = sem("s_xin"), sem("s_bw"), [sem("s_b0"), sem("s_b1")], sem("s_c")
        s_xrl = [sem(f"s_xrl{n}") for n in range(NX)]
        s_xrs = [sem(f"s_xrs{n}") for n in range(NX)]
        (s_xn, s_inp, s_row, s_rowev, s_vev, s_hin, s_hout, s_tap0, s_tap, s_silu, s_xp, s_xd, s_dt,
         s_abs, s_relu, s_e, s_l, s_w1, s_w3, s_delta, s_du, s_dbu, s_da, s_scan, s_scp, s_cm,
         s_ns1, s_ns2, s_y, s_sq, s_ln, s_ls, s_mean, s_msq, s_e2, s_var, s_vare, s_lv, s_rs0, s_nt,
         s_rstd, s_op, s_ov, s_xrb, s_x1, s_bn, s_pad) = (sem("q_" + n) for n in (
             "xn inp row rowev vev hin hout tap0 tap silu xp xd dt abs relu e l w1 w3 delta du dbu da "
             "scan scp cm ns1 ns2 y sq ln ls mean msq e2 var vare lv rs0 nt rstd op ov xrb x1 bn pad").split())

        L_CONV, L_DT, L_SP, L_CH, L_SCAN, L_Y, L_SQ = 2, 14, 15, 16, 17, 18, 19
        S_LN, S_OP = 30, 31
        SLOTS = 12 * (NCH - 1) + S_OP + XT + 3

        def tile(S, lag):
            i = S - lag
            return i if 0 <= i < NT else None

        def chunk_at(S, rel):
            c, r = divmod(S - rel, K)
            return c if r == 0 and 0 <= c < NCH else None

        def proj_at(S, rel):
            c, m = divmod(S - rel, K)
            return (c, m) if m < XT and 0 <= c < NCH else (None, None)

        def houts(i):
            if i < 0:
                return 0
            b, r = divmod(i, CPB * K)
            return b * (CPB - 1) * K + min(r + 1, (CPB - 1) * K)

        def first_rows(i):
            b, r = divmod(i, CPB * K)
            return b * K + min(r + 1, K)

        def cols_of(c):
            k = c % CPB
            lo = 0 if k == 0 else (ROWS * k + 1) * W
            hi = T if k == CPB - 1 else (ROWS * (k + 1) + 1) * W
            return lo, hi

        def ucol(i):
            return UY[:, (i // K) % NU, i % K, :]

        TAPS = [(dy, dx) for dy in range(3) for dx in range(3) if (dy, dx) != (1, 1)]

        def win_view(i, dy, dx):
            return VS[:, i % NV, dy:dy + ROWS, dx:dx + W]

        def rows(ap):
            return ap.rearrange("p (r w) -> p r w", w=W)

        with nc.Block() as block:
            @block.sync
            def _(sp):
                def load_win(i):
                    if i < NT:
                        wait(sp, s_inp, i - NW + 1)
                        sp.dma_start(WR[:, i % NW], g["win"][i % K]).then_inc(s_win[i % NW], 16)

                def load_wout(r):
                    if r < 2 * XT * NCH:
                        wait(sp, s_op, r - 3 + 1)
                        m, h = divmod(r % (2 * XT), 2)
                        sp.dma_start(OR[:, r % 3], woc_d[m, :, h * HALF:(h + 1) * HALF, :])\
                          .then_inc(s_wor[r % 3], 16)

                def load_xr(r):
                    if r < XT * NCH:
                        c, m = divmod(r, XT)
                        b, k = divmod(c, CPB)
                        if r >= NX:
                            sp.wait_ge(s_xrs[r % NX], 16 * (r // NX))
                            sp.wait_ge(s_bn, r - NX + 1)
                        sp.dma_start(XR[:, r % NX, :], XTR[b, :, m, k * N:(k + 1) * N])\
                          .then_inc(s_xrl[r % NX], 16)

                for i in range(NW - 1):
                    load_win(i)
                for r in range(2):
                    load_wout(r)
                for S in range(SLOTS):
                    if S % K == 0 and S < NT:
                        c = S // K
                        lo, hi = cols_of(c)
                        wait(sp, s_inp, K * c)
                        sp.dma_start(XN[:, :, 0:hi - lo], XTR[c // CPB, :, :, lo:hi]).then_inc(s_xin, 16)
                    load_win(S + NW - 1)
                    c = chunk_at(S, 14)
                    if c is not None:
                        sp.wait_ge(s_xd, c + 1)
                        sp.dma_start(bc_d[c], XD[R:R + 2 * NS, :]).then_inc(s_bw, 16)
                        sp.wait_ge(s_bw, 16 * (c + 1))
                        wait(sp, s_dbu, K * (c - 1))
                        sp.dma_start(BB[:, c % 2].rearrange("p n t -> p (n t)"),
                                     bc_d[c, 0:NS].rearrange("n t -> (n t)").partition_broadcast(P))\
                          .then_inc(s_b[c % 2], 16)
                    c = chunk_at(S, 16)
                    if c is not None:
                        wait(sp, s_cm, K * c)
                        sp.dma_start(CB[:].rearrange("p n t -> p (n t)"),
                                     bc_d[c, NS:2 * NS].rearrange("n t -> (n t)").partition_broadcast(P))\
                          .then_inc(s_c, 16)
                    c, m = proj_at(S, S_OP + 2)
                    if c is not None:
                        r = c * XT + m
                        b, k = divmod(c, CPB)
                        sp.wait_ge(s_x1, r + 1)
                        sp.dma_start(x1_d[b, :, m, k * N:(k + 1) * N], XR[:, r % NX, :])\
                          .then_inc(s_xrs[r % NX], 16)
                    c, m = proj_at(S, S_OP - 1)
                    if c is not None:
                        load_xr(c * XT + m)
                    c, m = proj_at(S, S_OP)
                    if c is not None:
                        r = c * XT + m
                        load_wout(2 * r + 2)
                        load_wout(2 * r + 3)
                for n in range(NX):
                    sp.wait_ge(s_xrs[n], 16 * ((XT * NCH - n + NX - 1) // NX))

            @block.tensor
            def _(pe):
                for S in range(SLOTS):
                    i = tile(S, 0)
                    if i is not None:
                        c, j = divmod(i, K)
                        lo, hi = cols_of(c)
                        pe.wait_ge(s_win[i % NW], 16 * (i // NW + 1))
                        pe.wait_ge(s_xn, c + 1)
                        wait(pe, s_vev, i)
                        off = 0
                        if c % CPB == 0:
                            off = W
                            for t in range(XT):
                                last = nc.tensor.matmul(p_in[:, 0:W], WR[:, i % NW, t, :], XN[:, t, 0:W],
                                                        start=(t == 0), stop=(t == XT - 1))
                            last.then_inc(s_row, 1)
                            pe.wait_ge(s_rowev, first_rows(i))
                        n = hi - lo - off
                        for t in range(XT):
                            last = nc.tensor.matmul(p_in[:, 0:n], WR[:, i % NW, t, :], XN[:, t, off:off + n],
                                                    start=(t == 0), stop=(t == XT - 1))
                        last.then_inc(s_inp, 1)
                    i = tile(S, L_SQ)
                    if i is not None:
                        c, j = divmod(i, K)
                        if j == 0:
                            wait(pe, s_ls, c)
                        q = j % 2
                        pe.wait_ge(s_y, i + 1)
                        nc.tensor.matmul(p_ln[64 + 32 * q:96 + 32 * q, :], ones32[:], ucol(i),
                                         start=(j < 2), stop=(j >= K - 2))
                        pe.wait_ge(s_sq, i + 1)
                        nc.tensor.matmul(p_ln[32 * q:32 * q + 32, :], ones32[:], SQ[:],
                                         start=(j < 2), stop=(j >= K - 2)).then_inc(s_ln, 1)
                    c = chunk_at(S, S_LN)
                    if c is not None:
                        pe.wait_ge(s_ls, c + 1)
                        wait(pe, s_xd, min(c + 2, NCH))
                        nc.tensor.matmul(p_ms[:], pick[:, 1, :], LS[:], start=True, stop=True).then_inc(s_mean, 1)
                    c, m = proj_at(S, S_OP)
                    if c is not None:
                        if m == 0:
                            pe.wait_ge(s_msq, c + 1)
                            nc.tensor.matmul(p_ms[:], pick[:, 0, :], LS[:], start=True, stop=True)\
                              .then_inc(s_e2, 1)
                            pe.wait_ge(s_var, c + 1)
                        r = c * XT + m
                        wait(pe, s_ov, r)
                        for h in range(2):
                            e = 2 * r + h
                            pe.wait_ge(s_wor[e % 3], 16 * (e // 3 + 1))
                            for k in range(HALF):
                                last = nc.tensor.matmul(p_ms[:], OR[:, e % 3, k, :],
                                                        UY[:, c % NU, h * HALF + k, :],
                                                        start=(h == 0 and k == 0), stop=(h == 1 and k == HALF - 1))
                            last.then_inc(s_op, 1)
                    c = chunk_at(S, 14)
                    if c is not None:
                        pe.wait_ge(s_silu, 3 * (c + 1))
                        wait(pe, s_ov, XT * (c - 1))
                        for k in range(K):
                            last = nc.tensor.matmul(p_ms[0:R + 2 * NS, :], xpt[:, k, :], UY[:, c % NU, k, :],
                                                    start=(k == 0), stop=(k == K - 1))
                        last.then_inc(s_xp, 1)
                    i = tile(S, L_DT)
                    if i is not None:
                        c, j = divmod(i, K)
                        pe.wait_ge(s_xd, c + 1)
                        wait(pe, s_relu, i)
                        nc.tensor.matmul(p_dt[:], dtt[:, j * P:(j + 1) * P], XD[0:R, :], start=True, stop=True)\
                          .then_inc(s_dt, 1)

            @block.scalar
            def _(act):
                nc.scalar.preload_act_table_set(EXPSET)
                act.wait_ge(s_pad, 1)

                def load_norm(c):
                    lo, hi = cols_of(c)
                    act.wait_ge(s_xin, 16 * (c + 1))
                    b = c // CPB
                    o = XN[:, :, 0:hi - lo]
                    nc.scalar.activation(o, o, ACT.Identity, bias=gbi[:, b:b + 1], scale=gsc[:, b:b + 1])\
                      .then_inc(s_xn, 1)

                def decay(i, n):
                    j, e = i % K, NS * i + n
                    act.wait_ge(s_delta, i + 1)
                    wait(act, s_scan, e - NDA + 1)
                    nc.scalar.activation(p_da[:, e % NDA, :], RR[:, i % 2, :], ACT.Exp,
                                         scale=At[:, j * NS + n:j * NS + n + 1]).then_inc(s_da, 1)

                for S in range(SLOTS):
                    i = tile(S, L_CONV)
                    if i is not None:
                        j = i % K
                        act.wait_ge(s_vev, i + 1)
                        act.wait_ge(s_hin, i + 1)
                        wait(act, s_rowev, first_rows(i))
                        wait(act, s_tap, len(TAPS) * i)
                        nc.scalar.activation(rows(p_cv[:]), win_view(i, 1, 1), ACT.Identity,
                                             bias=convb[:, j:j + 1], scale=cwt[:, j, 4:5]).then_inc(s_tap0, 1)
                    i = tile(S, L_SCAN)
                    if i is not None:
                        decay(i, NS - 1)
                    if S % K == 0 and S < NT:
                        load_norm(S // K)
                    i = tile(S, 0)
                    if i is not None:
                        c = i // K
                        wait(act, s_tap, len(TAPS) * (i - NV + 1))
                        wait(act, s_hout, houts(i - NV))
                        if c % CPB == 0:
                            act.wait_ge(s_row, first_rows(i))
                            nc.scalar.activation(VS[:, i % NV, 1, 1:1 + W], p_in[:, 0:W], ACT.Copy)\
                              .then_inc(s_rowev, 1)
                        act.wait_ge(s_inp, i + 1)
                        nr = ROWS - 1 if c % CPB == CPB - 1 else ROWS
                        nc.scalar.activation(VS[:, i % NV, 2:2 + nr, 1:1 + W], rows(p_in[:, 0:nr * W]), ACT.Copy)\
                          .then_inc(s_vev, 1)
                    i = tile(S, L_SQ)
                    if i is not None:
                        act.wait_ge(s_y, i + 1)
                        wait(act, s_ln, i)
                        nc.scalar.activation(SQ[:], ucol(i), ACT.Square).then_inc(s_sq, 1)
                    i = tile(S, L_SP)
                    if i is not None:
                        j, h = i % K, i % 2
                        act.wait_ge(s_dt, i + 1)
                        wait(act, s_delta, i)
                        nc.scalar.activation(EE[:], p_dt[:], ACT.Abs, bias=dtb[:, j:j + 1]).then_inc(s_abs, 1)
                        wait(act, s_dbu, i - 1)
                        wait(act, s_da, NS * (i - 1))
                        nc.scalar.activation(RR[:, h, :], p_dt[:], ACT.Relu, bias=dtb[:, j:j + 1]).then_inc(s_relu, 1)
                        act.wait_ge(s_abs, i + 1)
                        nc.scalar.activation(EE[:], EE[:], ACT.Exp, scale=-1.0).then_inc(s_e, 1)
                        act.wait_ge(s_e, i + 1)
                        nc.scalar.activation(LL[:], EE[:], ACT.Ln, bias=1.0).then_inc(s_l, 1)
                    if S >= 6 and S % 4 == 2 and (S - 6) // 4 < NT // 4:
                        q = (S - 6) // 4
                        act.wait_ge(s_tap, len(TAPS) * 4 * (q + 1))
                        o = UY[:, (q // 3) % NU, (q % 3) * 4:(q % 3) * 4 + 4, :]
                        nc.scalar.activation(o, o, ACT.Silu).then_inc(s_silu, 1)
                        nc.scalar.preload_act_table_set(EXPSET)
                    c = chunk_at(S, 14)
                    if c is not None:
                        act.wait_ge(s_xp, c + 1)
                        wait(act, s_dt, K * c)
                        wait(act, s_bw, 16 * c)
                        nc.scalar.activation(XD[:], p_ms[0:R + 2 * NS, :], ACT.Copy).then_inc(s_xd, 1)
                    c = chunk_at(S, S_OP)
                    if c is not None:
                        act.wait_ge(s_mean, c + 1)
                        nc.scalar.activation(MS[:], p_ms[:], ACT.Square).then_inc(s_msq, 1)
                        act.wait_ge(s_vare, c + 1)
                        wait(act, s_ov, XT * c)
                        nc.scalar.activation(RS[:], MS[:], ACT.Ln).then_inc(s_lv, 1)
                        act.wait_ge(s_lv, c + 1)
                        nc.scalar.activation(RS[:], RS[:], ACT.Exp, scale=-0.5).then_inc(s_rs0, 1)
                    c = chunk_at(S, S_LN)
                    if c is not None:
                        act.wait_ge(s_ln, K * (c + 1))
                        nc.scalar.activation(LS[:], p_ln[:], ACT.Copy).then_inc(s_ls, 1)
                    c, m = proj_at(S, S_OP)
                    if c is not None:
                        r = c * XT + m
                        act.wait_ge(s_xrl[r % NX], 16 * (r // NX + 1))
                        o = XR[:, r % NX, :]
                        nc.scalar.activation(o, o, ACT.Identity, bias=bm[:, m:m + 1]).then_inc(s_xrb, 1)
                    i = tile(S, L_CH)
                    if i is not None:
                        for n in range(NS - 1):
                            decay(i, n)

            @block.gpsimd
            def _(pool):
                nc.gpsimd.memset(VS[:], 0.0).then_inc(s_pad, 1)
                pool.wait_ge(s_pad, 1)
                for S in range(SLOTS):
                    i = tile(S, L_Y)
                    if i is not None:
                        gi = G[:, i % NG]
                        pool.wait_ge(s_cm, i + 1)
                        nc.gpsimd.tensor_tensor(gi[:, 0:2], gi[:, 0:2], gi[:, 2:4], ALU.add).then_inc(s_ns1, 1)
                        pool.wait_ge(s_ns1, i + 1)
                        nc.gpsimd.tensor_tensor(gi[:, 0], gi[:, 0], gi[:, 1], ALU.add).then_inc(s_ns2, 1)
                    i = tile(S, L_CH)
                    if i is not None:
                        c, j = divmod(i, K)
                        h = i % 2
                        pool.wait_ge(s_l, i + 1)
                        wait(pool, s_dbu, i)
                        nc.gpsimd.tensor_scalar(TM[:], EE[:], 1.0, 1.0, ALU.add, ALU.subtract).then_inc(s_w1, 1)
                        pool.wait_ge(s_w1, 2 * i + 1)
                        nc.gpsimd.tensor_tensor(TM[:], EE[:], TM[:], ALU.subtract).then_inc(s_w1, 1)
                        nc.gpsimd.tensor_tensor(RR[:, h, :], RR[:, h, :], LL[:], ALU.add).then_inc(s_w3, 1)
                        pool.wait_ge(s_w1, 2 * i + 2)
                        pool.wait_ge(s_w3, i + 1)
                        nc.gpsimd.tensor_tensor(RR[:, h, :], RR[:, h, :], TM[:], ALU.add).then_inc(s_delta, 1)
                        pool.wait_ge(s_delta, i + 1)
                        nc.gpsimd.tensor_tensor(TM[:], RR[:, h, :], ucol(i), ALU.mult).then_inc(s_du, 1)
                        pool.wait_ge(s_du, i + 1)
                        wait(pool, s_y, i - NG + 1)
                        pool.wait_ge(s_b[c % 2], 16 * (c // 2 + 1))
                        nc.gpsimd.tensor_tensor(G[:, i % NG], TM[:].unsqueeze(1).broadcast_to([P, NS, N]),
                                                BB[:, c % 2], ALU.mult).then_inc(s_dbu, 1)
                    i = tile(S, 0)
                    if i is not None:
                        k, j = (i // K) % CPB, i % K
                        wait(pool, s_tap, len(TAPS) * (i - NV + 1))
                        if k == 0:
                            last = nc.gpsimd.memset(VS[:, i % NV, 0, :], 0.0)
                        else:
                            pool.wait_ge(s_hout, houts(i - K))
                            last = nc.gpsimd.tensor_copy(VS[:, i % NV, 0:2, 1:1 + W], HA[:, j])
                            if k == CPB - 1:
                                wait(pool, s_hout, houts(i - NV))
                                last = nc.gpsimd.memset(VS[:, i % NV, ROWS + 1, :], 0.0)
                        last.then_inc(s_hin, 1)
                        if k < CPB - 1:
                            pool.wait_ge(s_vev, i + 1)
                            pool.wait_ge(s_hin, i + 1)
                            nc.gpsimd.tensor_copy(HA[:, j], VS[:, i % NV, ROWS:ROWS + 2, 1:1 + W]).then_inc(s_hout, 1)
                    c = chunk_at(S, S_OP)
                    if c is not None:
                        pool.wait_ge(s_var, c + 1)
                        nc.gpsimd.tensor_scalar(MS[:], MS[:], 0.0, 1e-5, ALU.max, ALU.add).then_inc(s_vare, 1)
                        pool.wait_ge(s_rs0, c + 1)
                        for q, (o, a, b2) in enumerate(((LS, RS, RS), (LS, LS, MS), (LS, None, None), (RS, RS, LS))):
                            if q:
                                pool.wait_ge(s_nt, 3 * c + q)
                            if a is None:
                                op = nc.gpsimd.tensor_scalar(o[:], o[:], -0.5, 1.5, ALU.mult, ALU.add)
                            else:
                                op = nc.gpsimd.tensor_tensor(o[:], a[:], b2[:], ALU.mult)
                            op.then_inc(s_nt if q < 3 else s_rstd, 1)
                    c, m = proj_at(S, S_OP + 1)
                    if c is not None:
                        r = c * XT + m
                        pool.wait_ge(s_ov, r + 1)
                        pool.wait_ge(s_xrb, r + 1)
                        o = XR[:, r % NX, :]
                        nc.gpsimd.tensor_tensor(o, o, TO[:], ALU.add).then_inc(s_x1, 1)

            @block.vector
            def _(vec):
                def scan(i, n):
                    c, j = divmod(i, K)
                    e = NS * i + n
                    vec.wait_ge(s_dbu, i + 1)
                    vec.wait_ge(s_da, e + 1)
                    init = 0.0
                    if c % CPB:
                        vec.wait_ge(s_scp, i - K + 1)
                        init = ST[:, j, n:n + 1]
                    gn = G[:, i % NG, n, :]
                    nc.vector.tensor_tensor_scan(gn, p_da[:, e % NDA, :], gn, init, ALU.mult, ALU.add)\
                      .then_inc(s_scan, 1)

                def keep_state(i):
                    vec.wait_ge(s_scan, NS * (i + 1))
                    nc.vector.tensor_copy(ST[:, i % K, :], G[:, i % NG, :, N - 1]).then_inc(s_scp, 1)

                def times_c(i):
                    vec.wait_ge(s_scp, i + 1)
                    vec.wait_ge(s_c, 16 * (i // K + 1))
                    gi = G[:, i % NG]
                    nc.vector.tensor_tensor(gi, gi, CB[:], ALU.mult).then_inc(s_cm, 1)

                def tap(i, q):
                    dy, dx = TAPS[q]
                    c, j = divmod(i, K)
                    if q == 0:
                        vec.wait_ge(s_tap0, i + 1)
                    else:
                        vec.wait_ge(s_tap, len(TAPS) * i + q)
                    dst = p_cv[:]
                    if q == len(TAPS) - 1:
                        dst = ucol(i)
                        wait(vec, s_op, 2 * XT * (c - NU + 1))
                    nc.vector.scalar_tensor_tensor(rows(dst), win_view(i, dy, dx),
                                                   cwt[:, j, 3 * dy + dx:3 * dy + dx + 1],
                                                   rows(p_cv[:]), ALU.mult, ALU.add).then_inc(s_tap, 1)

                def skip_add(i):
                    vec.wait_ge(s_ns2, i + 1)
                    vec.wait_ge(s_du, i + 1)
                    nc.vector.scalar_tensor_tensor(ucol(i), ucol(i), Dp[:, i % K:i % K + 1], G[:, i % NG, 0, :],
                                                   ALU.mult, ALU.add).then_inc(s_y, 1)

                for S in range(SLOTS):
                    a, b, y = tile(S, L_SCAN), tile(S, L_CONV), tile(S, L_Y)
                    for n in range(NS):
                        if a is not None:
                            scan(a, n)
                        if b is not None:
                            tap(b, n)
                    if a is not None:
                        keep_state(a)
                    if b is not None:
                        tap(b, 4)
                    if a is not None:
                        times_c(a)
                    if b is not None:
                        tap(b, 5)
                    if y is not None:
                        skip_add(y)
                    if b is not None:
                        tap(b, 6)
                    c, m = proj_at(S, S_OP + 2)
                    if c is not None:
                        r = c * XT + m
                        bb, k = divmod(c, CPB)
                        vec.wait_ge(s_x1, r + 1)
                        nc.vector.bn_stats(stats1[:, bb, m * CPB + k, :], XR[:, r % NX, :]).then_inc(s_bn, 1)
                    c, m = proj_at(S, S_OP + 1)
                    if c is not None:
                        r = c * XT + m
                        vec.wait_ge(s_op, 2 * r + 2)
                        vec.wait_ge(s_rstd, c + 1)
                        wait(vec, s_x1, r)
                        nc.vector.tensor_tensor(TO[:], p_ms[:], RS[:], ALU.mult).then_inc(s_ov, 1)
                    if b is not None:
                        tap(b, 7)
                    c = chunk_at(S, S_OP)
                    if c is not None:
                        vec.wait_ge(s_e2, c + 1)
                        nc.vector.tensor_tensor(MS[:], p_ms[:], MS[:], ALU.subtract).then_inc(s_var, 1)


def layer1(nc, g):
    (B, C, T, N, CPB, XT) = (g[n] for n in "B C T N CPB XT".split())
    x1_d, OUTR = g["x1_d"], g["OUTR"]
    quad, gsc, gbi, stats1, gtmp = g["quad"], g["gsc"], g["gbi"], g["stats1"], g["gtmp"]
    NH = 12
    TB = N // P
    with ExitStack() as ctx:
        def sb(name, shape):
            return ctx.enter_context(nc.sbuf_tensor(name, shape, F32))

        def ps(name, shape):
            return ctx.enter_context(nc.psum_tensor(name, shape, F32))

        WQ = sb("wqkv", [P, XT, C])
        WO = sb("wo", [P, XT, C])
        WA = sb("wo_attn", [P, XT, C])
        XC = sb("xc", [P, 2, XT, N])
        WW = sb("w_all", [P, XT, T])
        W2 = sb("w_sq", [P, XT, N])
        JK = sb("junk", [P, 2, N])
        n2 = sb("n2", [P, XT, CPB])
        dn = sb("dn", [P, XT, CPB])
        small = sb("small", [P, 8, XT])
        tmpc = sb("tmpc", [P, XT])
        sel = sb("sel", [P, XT, NH])
        lsel = sb("lsel", [P, XT, NH])
        selb = sb("selb", [NH, C])
        ident = sb("ident", [P, P])
        mx = sb("mx", [P, 4, TB])
        lz = sb("lz", [P, TB, NH])
        pi = sb("pi", [P, TB, NH])
        PT = sb("pi_t", [NH, N])
        sh = sb("sh", [NH, CPB + 1])

        p_w = ps("p_w", [P, 2, N])
        p_lg = ps("p_lg", [P, N])
        p_pt = ps("p_pt", [P, N])
        p_pb = ps("p_pb", [P, 2, N])
        p_sm = ps("p_sm", [P, N])

        def sem(name):
            return ctx.enter_context(nc.semaphore(name))

        s_par, s_gv, s_gp, s_ga = sem("t_par"), sem("t_gv"), sem("t_gp"), sem("t_ga")
        s_xl = [sem("t_xl0"), sem("t_xl1")]
        s_os = [sem("t_os0"), sem("t_os1")]
        (s_xn, s_qk, s_cp, s_ss, s_n2, s_lsel, s_w2, s_lg, s_mx, s_lz, s_ez, s_pi, s_tp, s_pt, s_pb, s_q,
         s_dn, s_sp, s_fin, s_wa, s_o, s_oe, s_sh) = (sem("t_" + n) for n in (
             "xn qk cp ss n2 lsel w2 lg mx lz ez pi tp pt pb q dn sp fin wa o oe sh").split())
        params = [(WQ[:], g["wqkv"]), (WO[:], g["wo2"]), (tmpc[:], g["temp"]), (sel[:], g["sel_d"]),
                  (selb[:], g["selb_d"]), (ident[:], g["ident_d"])]
        NP_ = 16 * len(params)
        NM, NF = 3, 6

        def steps(b):
            return group_norm_scale(nc.vector, nc.tensor, nc.scalar, nc, (s_gv, s_gp, s_ga),
                                    stats1[:, b], CPB * XT, gtmp, p_sm, quad[:], 1e-5,
                                    gsc[:, B + b:B + b + 1], gbi[:, B + b:B + b + 1])

        with nc.Block() as block:
            def store(sp, b, k):
                cc = b * CPB + k
                sp.wait_ge(s_oe, XT * (cc + 1))
                sp.dma_start(OUTR[b, :, :, k * N:(k + 1) * N], XC[:, k % 2]).then_inc(s_os[k % 2], 16)

            @block.sync
            def _(sp):
                for dst, src in params:
                    sp.dma_start(dst, src).then_inc(s_par, 16)
                for b in range(B):
                    for ph in range(2):
                        for k in range(CPB):
                            u = (2 * b + ph) * CPB + k
                            cc = b * CPB + k
                            if k >= 2:
                                if ph == 0:
                                    sp.wait_ge(s_qk, XT * (cc - 1))
                                else:
                                    sp.wait_ge(s_os[u % 2], 16 * ((b * CPB + k - 2) // 2 + 1))
                            elif ph == 1:
                                sp.wait_ge(s_qk, XT * (b * CPB + CPB))
                            elif b > 0:
                                sp.wait_ge(s_os[u % 2], 16 * (b * CPB // 2))
                            sp.dma_start(XC[:, u % 2], x1_d[b, :, :, k * N:(k + 1) * N]).then_inc(s_xl[u % 2], 16)
                            if ph == 1 and k >= 1:
                                store(sp, b, k - 1)
                    store(sp, b, CPB - 1)
                for n in range(2):
                    sp.wait_ge(s_os[n], 16 * (B * CPB // 2))

            @block.tensor
            def _(pe):
                pe.wait_ge(s_par, NP_)
                for b in range(B):
                    steps(b)[1](b * GN_V, b * GN_P, b * GN_A)
                for b in range(B):
                    wait(pe, s_oe, XT * CPB * b)
                    for k in range(CPB):
                        cc = b * CPB + k
                        u = 2 * b * CPB + k
                        pe.wait_ge(s_xn, cc + 1)
                        for t in range(XT):
                            n = XT * cc + t
                            wait(pe, s_cp, n - 1)
                            for q in range(XT):
                                last = nc.tensor.matmul(p_w[:, n % 2, :], WQ[:, q, t * P:(t + 1) * P],
                                                        XC[:, u % 2, q, :], start=(q == 0), stop=(q == XT - 1))
                            last.then_inc(s_qk, 1)
                    pe.wait_ge(s_lsel, b + 1)
                    for k in range(CPB):
                        cc = b * CPB + k
                        pe.wait_ge(s_w2, cc + 1)
                        wait(pe, s_lz, cc)
                        for tb in range(TB):
                            for t in range(XT):
                                last = nc.tensor.matmul(p_lg[:, tb * NH:(tb + 1) * NH],
                                                        W2[:, t, tb * P:(tb + 1) * P], lsel[:, t, :],
                                                        start=(t == 0), stop=(t == XT - 1))
                        last.then_inc(s_lg, 1)
                        pe.wait_ge(s_pi, cc + 1)
                        wait(pe, s_pt, cc)
                        for tb in range(TB):
                            last = nc.tensor.transpose(p_pt[0:NH, tb * P:(tb + 1) * P], pi[:, tb, :], ident[:])
                        last.then_inc(s_tp, 1)
                        pe.wait_ge(s_pt, cc + 1)
                        for t in range(XT):
                            n = XT * cc + t
                            wait(pe, s_q, n - 1)
                            wait(pe, s_dn, n - 1)
                            nc.tensor.matmul(p_pb[:, n % 2, :], selb[:, t * P:(t + 1) * P], PT[:],
                                             start=True, stop=True).then_inc(s_pb, 1)
                    pe.wait_ge(s_sh, b + 1)
                    for t in range(XT):
                        last = nc.tensor.matmul(p_sm[:, 8 + t:9 + t], selb[:, t * P:(t + 1) * P],
                                                sh[:, CPB:CPB + 1], start=True, stop=True)
                    last.then_inc(s_sp, 1)
                    pe.wait_ge(s_wa, XT * (b + 1))
                    for k in range(CPB):
                        cc = b * CPB + k
                        for m in range(XT):
                            n = XT * cc + m
                            wait(pe, s_oe, n - 1)
                            for q in range(XT):
                                last = nc.tensor.matmul(p_w[:, n % 2, :], WA[:, q, m * P:(m + 1) * P],
                                                        WW[:, q, k * N:(k + 1) * N],
                                                        start=(q == 0), stop=(q == XT - 1))
                            last.then_inc(s_o, 1)

            @block.scalar
            def _(act):
                nc.scalar.preload_act_table_set(EXPSET)
                for b in range(B):
                    steps(b)[2](b * GN_V, b * GN_P, b * GN_A)
                for b in range(B):
                    act.wait_ge(s_gv, GN_V * B)
                    for k in range(CPB + 1):
                        cc = b * CPB + k
                        if k < CPB:
                            u = 2 * b * CPB + k
                            act.wait_ge(s_xl[u % 2], 16 * (u // 2 + 1))
                            o = XC[:, u % 2]
                            nc.scalar.activation(o, o, ACT.Identity, bias=gbi[:, B + b:B + b + 1],
                                                 scale=gsc[:, B + b:B + b + 1]).then_inc(s_xn, 1)
                        if k >= 1:
                            for t in range(XT):
                                n = XT * (cc - 1) + t
                                act.wait_ge(s_cp, n + 1)
                                wait(act, s_ss, n - 1)
                                nc.scalar.activation(JK[:, n % 2, :], WW[:, t, (k - 1) * N:k * N], ACT.Square,
                                                     accum_out=n2[:, t, k - 1:k]).then_inc(s_ss, 1)
                    for k in range(CPB):
                        cc = b * CPB + k
                        wait(act, s_lg, cc)
                        wait(act, s_dn, XT * cc)
                        act.wait_ge(s_cp, XT * CPB * (b + 1))
                        nc.scalar.activation(W2[:], WW[:, :, k * N:(k + 1) * N], ACT.Square).then_inc(s_w2, 1)
                        act.wait_ge(s_lz, cc + 1)
                        nc.scalar.activation(lz[:], lz[:], ACT.Exp).then_inc(s_ez, 1)
                        act.wait_ge(s_tp, cc + 1)
                        wait(act, s_pb, XT * cc)
                        nc.scalar.activation(PT[:], p_pt[0:NH, :], ACT.Copy, accum_out=sh[:, k:k + 1])\
                          .then_inc(s_pt, 1)
                    act.wait_ge(s_fin, NF * (b + 1))
                    for q in range(XT):
                        wait(act, s_o, XT * CPB * b)
                        nc.scalar.activation(WA[:, q, :], WO[:, q, :], ACT.Copy, scale=small[:, 5, q:q + 1])\
                          .then_inc(s_wa, 1)

            @block.vector
            def _(vec):
                for b in range(B):
                    wait(vec, s_gv, GN_V * b)
                    steps(b)[0](b * GN_V, b * GN_P, b * GN_A)
                vec.wait_ge(s_par, NP_)
                for b in range(B):
                    for k in range(CPB):
                        cc = b * CPB + k
                        for t in range(XT):
                            n = XT * cc + t
                            vec.wait_ge(s_qk, n + 1)
                            if b:
                                vec.wait_ge(s_o, XT * CPB * b)
                            nc.vector.tensor_copy(WW[:, t, k * N:(k + 1) * N], p_w[:, n % 2, :]).then_inc(s_cp, 1)
                    vec.wait_ge(s_ss, XT * CPB * (b + 1))
                    nc.vector.reduce_sum(small[:, 0, :], n2[:], AX.X).then_inc(s_n2, 1)
                    vec.wait_ge(s_n2, 4 * b + 1)
                    nc.vector.tensor_scalar(small[:, 0, :], small[:, 0, :], 1e-24, None, ALU.max).then_inc(s_n2, 1)
                    vec.wait_ge(s_n2, 4 * b + 2)
                    nc.vector.reciprocal(small[:, 1, :], small[:, 0, :]).then_inc(s_n2, 1)
                    vec.wait_ge(s_n2, 4 * b + 3)
                    nc.vector.tensor_mul(small[:, 6, :], small[:, 1, :], tmpc[:]).then_inc(s_n2, 1)
                    vec.wait_ge(s_n2, 4 * b + 4)
                    wait(vec, s_lg, CPB * b)
                    nc.vector.tensor_tensor(lsel[:], sel[:], small[:, 6, :].unsqueeze(2).broadcast_to([P, XT, NH]),
                                            ALU.mult).then_inc(s_lsel, 1)
                    for k in range(CPB):
                        cc = b * CPB + k
                        m0 = NM * cc
                        lg = p_lg[:, 0:TB * NH].rearrange("p (t h) -> p t h", h=NH)
                        vec.wait_ge(s_lg, cc + 1)
                        nc.vector.tensor_reduce(mx[:, 0, :], lg, AX.X, ALU.max).then_inc(s_mx, 1)
                        vec.wait_ge(s_mx, m0 + 1)
                        wait(vec, s_pi, cc)
                        nc.vector.tensor_tensor(lz[:], lg, mx[:, 0, :].unsqueeze(2).broadcast_to([P, TB, NH]),
                                                ALU.subtract).then_inc(s_lz, 1)
                        vec.wait_ge(s_ez, cc + 1)
                        nc.vector.reduce_sum(mx[:, 1, :], lz[:], AX.X).then_inc(s_mx, 1)
                        vec.wait_ge(s_mx, m0 + 2)
                        nc.vector.reciprocal(mx[:, 2, :], mx[:, 1, :]).then_inc(s_mx, 1)
                        vec.wait_ge(s_mx, m0 + 3)
                        wait(vec, s_tp, cc)
                        nc.vector.tensor_tensor(pi[:], lz[:], mx[:, 2, :].unsqueeze(2).broadcast_to([P, TB, NH]),
                                                ALU.mult).then_inc(s_pi, 1)
                        for t in range(XT):
                            n = XT * cc + t
                            vec.wait_ge(s_pb, n + 1)
                            wait(vec, s_dn, n - 1)
                            nc.vector.tensor_tensor_reduce(out=JK[:, n % 2, :], in0=W2[:, t, :], in1=p_pb[:, n % 2, :],
                                                           scale=1.0, scalar=0.0, op0=ALU.mult, op1=ALU.add,
                                                           accum_out=dn[:, t, k:k + 1]).then_inc(s_dn, 1)
                            o = WW[:, t, k * N:(k + 1) * N]
                            nc.vector.tensor_tensor(o, o, p_pb[:, n % 2, :], ALU.mult).then_inc(s_q, 1)
                    vec.wait_ge(s_pt, CPB * (b + 1))
                    nc.vector.reduce_sum(sh[:, CPB:CPB + 1], sh[:, 0:CPB], AX.X).then_inc(s_sh, 1)
                    f0 = NF * b
                    vec.wait_ge(s_dn, XT * CPB * (b + 1))
                    nc.vector.reduce_sum(small[:, 2, :], dn[:], AX.X).then_inc(s_fin, 1)
                    vec.wait_ge(s_sp, b + 1)
                    nc.vector.tensor_scalar(small[:, 3, :], p_sm[:, 8:8 + XT], 1e-8, None, ALU.add).then_inc(s_fin, 1)
                    vec.wait_ge(s_fin, f0 + 2)
                    nc.vector.reciprocal(small[:, 4, :], small[:, 3, :]).then_inc(s_fin, 1)
                    vec.wait_ge(s_fin, f0 + 3)
                    nc.vector.tensor_mul(small[:, 2, :], small[:, 2, :], small[:, 4, :]).then_inc(s_fin, 1)
                    vec.wait_ge(s_fin, f0 + 4)
                    nc.vector.tensor_scalar(small[:, 3, :], small[:, 2, :], -1.0, -1.0, ALU.mult, ALU.add)\
                      .then_inc(s_fin, 1)
                    vec.wait_ge(s_fin, f0 + 5)
                    nc.vector.reciprocal(small[:, 5, :], small[:, 3, :]).then_inc(s_fin, 1)
                    for k in range(CPB):
                        cc = b * CPB + k
                        u = (2 * b + 1) * CPB + k
                        vec.wait_ge(s_xl[u % 2], 16 * (u // 2 + 1))
                        for m in range(XT):
                            n = XT * cc + m
                            vec.wait_ge(s_o, n + 1)
                            o = XC[:, u % 2, m, :]
                            nc.vector.tensor_tensor(o, o, p_w[:, n % 2, :], ALU.add).then_inc(s_oe, 1)


def kernel(**inputs):
    import numpy as np
    import concourse.bacc as bacc
    from concourse.bass_utils import run_bass_kernel_spmd

    a = {n.replace("L0_conv_", "").replace("L1_conv_", "l1_"): np.asarray(v) for n, v in inputs.items()}
    C, DI = 768, 1536
    XT, K = C // P, DI // P
    NH = a["l1_temp"].shape[0]

    def col(v):
        return v.reshape(K, P).T

    head = np.arange(C) // (C // NH)
    pick = np.zeros((P, 2, P), np.float32)
    pick[:64, 0] = pick[64:, 1] = 1.0 / (32 * DI)
    arrays = {
        "x": a["x"],
        "win": a["in_proj_w"].reshape(K, P, P, XT).transpose(0, 2, 3, 1),
        "wout": a["out_proj_w"].T.reshape(K, P, P, XT).transpose(1, 0, 3, 2).reshape(P, K, C),
        "xpw": a["x_proj_w"].T.reshape(K, P, -1).transpose(1, 0, 2),
        "dtw": a["dt_w"][0].T,
        "cw": a["conv_w"].reshape(K, P, 9).transpose(1, 0, 2),
        "cols": np.stack([col(a["conv_b"]), col(a["dt_b"][0]), col(a["D_param"][0]), col(a["ln_g"]),
                          col(a["ln_b"])], axis=1),
        "alog": a["A_log"][0].reshape(K, P, -1).transpose(1, 0, 2).reshape(P, -1),
        "wqkv": a["l1_W_qkv"].T.reshape(P, XT, C),
        "wo2": a["l1_W_out"].T.reshape(XT, P, P, XT).transpose(1, 0, 3, 2).reshape(P, XT, C),
        "temp": a["l1_temp"][head, 0].reshape(XT, P).T,
        "quad_d": np.kron(np.eye(P // 4), np.full((4, 4), 0.25)).astype(np.float32),
        "pick_d": pick,
        "sel_d": (head.reshape(XT, P).T[:, :, None] == np.arange(NH)).astype(np.float32),
        "selb_d": (np.arange(NH)[:, None] == head).astype(np.float32),
        "ident_d": np.eye(P, dtype=np.float32),
    }
    arrays = {"in_" + n: np.ascontiguousarray(v) for n, v in arrays.items()}
    nc = bacc.Bacc("TRN2", target_bir_lowering=False, num_devices=1)
    args = [nc.dram_tensor(n, v.shape, mybir.dt.from_np(v.dtype), kind="ExternalInput").ap()
            for n, v in arrays.items()]
    out = nc.dram_tensor("out", a["x"].shape, F32, kind="ExternalOutput").ap()
    build(nc, *args, out)
    r = run_bass_kernel_spmd(nc, [arrays], core_ids=[0])
    return r.results[0]["out"]
```

```python
from contextlib import ExitStack

import concourse.bass as bass
from concourse import mybir
from concourse.alu_op_type import AluOpType as ALU

F32 = mybir.dt.float32
F32R = mybir.dt.float32r
ACT = mybir.ActivationFunctionType
AX = mybir.AxisListType

P = 128
EXPSET = "natural_log_exp_and_others"


def wait(eng, sem, value):
    if value > 0:
        eng.wait_ge(sem, value)


def group_norm_scale(vec, pe, act, nc, s, stats, nstat, tmp, psum, quad, eps, scale, bias):
    own, dev, mean_g, var_g = tmp[:, 0:2], tmp[:, 2:3], tmp[:, 3:4], tmp[:, 4:5]
    lg, half = tmp[:, 5:6], tmp[:, 6:7]
    v, p, a = s

    def vector_steps(v0, p0, a0):
        nc.vector.bn_aggr(own, stats.rearrange("p n s -> p (n s)")).then_inc(v, 1)
        vec.wait_ge(p, p0 + 1)
        nc.vector.tensor_copy(mean_g, psum[:, 0:1]).then_inc(v, 1)
        vec.wait_ge(v, v0 + 2)
        nc.vector.tensor_sub(dev, own[:, 0:1], mean_g).then_inc(v, 1)
        vec.wait_ge(v, v0 + 3)
        nc.vector.tensor_mul(dev, dev, dev).then_inc(v, 1)
        vec.wait_ge(v, v0 + 4)
        nc.vector.tensor_add(dev, dev, own[:, 1:2]).then_inc(v, 1)
        vec.wait_ge(p, p0 + 2)
        nc.vector.tensor_scalar(var_g, psum[:, 1:2], eps, None, ALU.add).then_inc(v, 1)
        vec.wait_ge(a, a0 + 2)
        nc.vector.tensor_mul(lg, half, half).then_inc(v, 1)
        vec.wait_ge(v, v0 + 7)
        nc.vector.tensor_mul(lg, lg, var_g).then_inc(v, 1)
        vec.wait_ge(v, v0 + 8)
        nc.vector.tensor_scalar(lg, lg, -0.5, 1.5, ALU.mult, ALU.add).then_inc(v, 1)
        vec.wait_ge(v, v0 + 9)
        nc.vector.tensor_mul(scale, lg, half).then_inc(v, 1)
        vec.wait_ge(v, v0 + 10)
        nc.vector.tensor_scalar(bias, mean_g, scale, -1.0, ALU.mult, ALU.mult).then_inc(v, 1)

    def tensor_steps(v0, p0, a0):
        pe.wait_ge(v, v0 + 1)
        nc.tensor.matmul(psum[:, 0:1], quad, own[:, 0:1], start=True, stop=True).then_inc(p, 1)
        pe.wait_ge(v, v0 + 5)
        nc.tensor.matmul(psum[:, 1:2], quad, dev, start=True, stop=True).then_inc(p, 1)

    def scalar_steps(v0, p0, a0):
        act.wait_ge(v, v0 + 6)
        nc.scalar.activation(lg, var_g, ACT.Ln).then_inc(a, 1)
        act.wait_ge(a, a0 + 1)
        nc.scalar.activation(half, lg, ACT.Exp, scale=-0.5).then_inc(a, 1)

    return vector_steps, tensor_steps, scalar_steps


GN_V, GN_P, GN_A = 11, 2, 2


def build(nc, x, win, wout, xpw, dtw, cw, cols, alog, wqkv, wo2, temp, quad_d, pick_d, sel_d, selb_d,
          ident_d, out):
    B, C, H, W = x.shape
    T = H * W
    ROWS = 8
    N = ROWS * W
    CPB = H // ROWS
    NCH = B * CPB
    XT = C // P
    K = win.shape[0]
    NT = NCH * K
    R = dtw.shape[0]
    NS = 4
    PW = W + 2
    XTR = x.rearrange("b (p t) h w -> b p t (h w)", t=XT)
    OUTR = out.rearrange("b (p t) h w -> b p t (h w)", t=XT)

    x1_d = nc.dram_tensor("x1_scratch", [B, P, XT, T], F32).ap()
    woc_d = nc.dram_tensor("wout_scratch", [XT, P, K, P], F32).ap()
    bc_d = nc.dram_tensor("bc_scratch", [NCH, 2 * NS, N], F32).ap()

    ws_d = nc.dram_tensor("wsplit_scratch", [2, XT, P, 2, C], F32).ap()

    with ExitStack() as keep:
        def sbk(name, shape):
            return keep.enter_context(nc.sbuf_tensor(name, shape, F32))

        quad = sbk("quad", [P, P])
        gsc = sbk("gsc", [P, 2 * B])
        gbi = sbk("gbi", [P, 2 * B])
        stats1 = sbk("stats1", [P, B, CPB * XT, 6])
        gtmp = sbk("gtmp", [P, 8])

        shared = dict(B=B, C=C, T=T, N=N, ROWS=ROWS, W=W, CPB=CPB, NCH=NCH, XT=XT, K=K, NT=NT, R=R, NS=NS, PW=PW,
                      XTR=XTR, OUTR=OUTR, x1_d=x1_d, woc_d=woc_d, bc_d=bc_d, ws_d=ws_d, quad=quad, gsc=gsc, gbi=gbi,
                      stats1=stats1, gtmp=gtmp, win=win, wout=wout, xpw=xpw, dtw=dtw, cw=cw, cols=cols,
                      alog=alog, wqkv=wqkv, wo2=wo2, temp=temp, quad_d=quad_d, pick_d=pick_d, sel_d=sel_d,
                      selb_d=selb_d, ident_d=ident_d)
        layer0(nc, shared)
        layer1(nc, shared)


def layer0(nc, g):
    (B, C, T, N, ROWS, W, CPB, NCH, XT, K, NT, R, NS, PW) = (
        g[n] for n in "B C T N ROWS W CPB NCH XT K NT R NS PW".split())
    XTR, x1_d, woc_d, bc_d = g["XTR"], g["x1_d"], g["woc_d"], g["bc_d"]
    quad, gsc, gbi, stats1, gtmp = g["quad"], g["gsc"], g["gbi"], g["stats1"], g["gtmp"]
    DI = K * P
    with ExitStack() as ctx:
        def sb(name, shape):
            return ctx.enter_context(nc.sbuf_tensor(name, shape, F32))

        cwt = sb("conv_w", [P, K, 9])
        colt = sb("cols", [P, 5, K])
        At = sb("A", [P, K * NS])
        xpt = sb("xproj_w", [P, K, R + 2 * NS])
        dtt = sb("dt_w", [64 + R, DI // 2])
        bm = sb("b_m", [P, XT])
        pick = sb("pick", [P, 2, P])
        ones32 = sb("ones32", [P, 32])
        convb, dtb, Dp, lng, lnb = (colt[:, n, :] for n in range(5))

        with ExitStack() as c0:
            NXR = 4
            xs = c0.enter_context(nc.sbuf_tensor("xstage", [P, NXR, T], F32))
            stats0 = c0.enter_context(nc.sbuf_tensor("stats0", [P, CPB * XT, 6], F32))
            wst = c0.enter_context(nc.sbuf_tensor("wstage", [P, K, C], F32))
            wsg = c0.enter_context(nc.sbuf_tensor("wscaled", [P, K, C], F32))
            avg = c0.enter_context(nc.sbuf_tensor("avg", [P, P], F32))
            pm = c0.enter_context(nc.psum_tensor("pm", [P, 2, 512], F32))
            pb = c0.enter_context(nc.psum_tensor("pb", [P, 512], F32))
            pg = c0.enter_context(nc.psum_tensor("pg", [P, 512], F32))
            s_par = c0.enter_context(nc.semaphore("s_par"))
            s_wst = c0.enter_context(nc.semaphore("s_wst"))
            s_xs = [c0.enter_context(nc.semaphore(f"s_xs{n}")) for n in range(NXR)]
            s_st = c0.enter_context(nc.semaphore("s_st"))
            s_gv = c0.enter_context(nc.semaphore("s_gv"))
            s_gp = c0.enter_context(nc.semaphore("s_gp"))
            s_ga = c0.enter_context(nc.semaphore("s_ga"))
            s_set = c0.enter_context(nc.semaphore("s_set"))
            s_wsg = c0.enter_context(nc.semaphore("s_wsg"))
            s_cm = c0.enter_context(nc.semaphore("s_colmean"))
            s_bmp = c0.enter_context(nc.semaphore("s_bmp"))
            s_cen = c0.enter_context(nc.semaphore("s_cen"))
            s_wod = c0.enter_context(nc.semaphore("s_wod"))
            s_A = c0.enter_context(nc.semaphore("s_A"))
            H2 = C // 2
            params = [(cwt[:], g["cw"]), (colt[:], g["cols"]), (At[:], g["alog"]), (xpt[:], g["xpw"]),
                      (dtt[0:R, :], g["dtw"][:, 0:DI // 2]), (dtt[64:64 + R, :], g["dtw"][:, DI // 2:DI]),
                      (quad[:], g["quad_d"]), (pick[:], g["pick_d"])]
            NB = T // 512
            with nc.Block() as block:
                @block.sync
                def _(sp):
                    for dst, src in params:
                        sp.dma_start(dst, src).then_inc(s_par, 16)
                    sp.dma_start(wst[:], g["wout"]).then_inc(s_wst, 16)
                    for t in range(XT):
                        wait(sp, s_st, NB * (t - NXR + 1))
                        sp.dma_start(xs[:, t % NXR, :], XTR[0, :, t, :]).then_inc(s_xs[t % NXR], 16)
                    sp.wait_ge(s_cen, 2 * K)
                    for m in range(XT):
                        sp.dma_start(woc_d[m], wsg[:, :, m * P:(m + 1) * P]).then_inc(s_wod, 16)
                    sp.wait_ge(s_wod, 16 * XT)

                norm_vector, norm_tensor, norm_scalar = group_norm_scale(
                    nc.vector, nc.tensor, nc.scalar, nc, (s_gv, s_gp, s_ga), stats0, NB * XT, gtmp, pg, quad[:],
                    1e-5, gsc[:, 0:1], gbi[:, 0:1])

                @block.vector
                def _(vec):
                    nc.vector.memset(avg[:], 1.0 / DI).then_inc(s_set, 1)
                    nc.vector.memset(ones32[:], 1.0).then_inc(s_set, 1)
                    for t in range(XT):
                        if t == XT - 2:
                            vec.wait_ge(s_cm, 2)
                            vec.wait_ge(s_wsg, K)
                            for k in range(K):
                                for h in range(2):
                                    o = wsg[:, k, h * H2:(h + 1) * H2]
                                    nc.vector.tensor_sub(o, o, pm[:, h, 0:H2]).then_inc(s_cen, 1)
                        vec.wait_ge(s_xs[t % NXR], 16 * (t // NXR + 1))
                        for q in range(NB):
                            nc.vector.bn_stats(stats0[:, t * NB + q, :],
                                               xs[:, t % NXR, q * 512:(q + 1) * 512]).then_inc(s_st, 1)
                    vec.wait_ge(s_par, 16 * len(params))
                    vec.wait_ge(s_st, NB * XT)
                    norm_vector(0, 0, 0)
                    vec.wait_ge(s_bmp, 1)
                    nc.vector.tensor_copy(bm[:], pb[:, 0:XT]).then_inc(s_set, 1)

                @block.scalar
                def _(act):
                    nc.scalar.preload_act_table_set(EXPSET)
                    act.wait_ge(s_par, 16 * len(params))
                    nc.scalar.activation(At[:], At[:], ACT.Exp).then_inc(s_A, 1)
                    act.wait_ge(s_A, 1)
                    nc.scalar.mul(At[:], At[:], -1.0).then_inc(s_A, 1)
                    act.wait_ge(s_wst, 16)
                    for k in range(K):
                        nc.scalar.activation(wsg[:, k, :], wst[:, k, :], ACT.Copy,
                                             scale=lng[:, k:k + 1]).then_inc(s_wsg, 1)
                    norm_scalar(0, 0, 0)

                @block.tensor
                def _(pe):
                    pe.wait_ge(s_set, 1)
                    pe.wait_ge(s_wsg, K)
                    for h in range(2):
                        for k in range(K):
                            last = nc.tensor.matmul(pm[:, h, 0:H2], avg[:], wsg[:, k, h * H2:(h + 1) * H2],
                                                    start=(k == 0), stop=(k == K - 1))
                        last.then_inc(s_cm, 1)
                    for m in range(XT):
                        for k in range(K):
                            last = nc.tensor.matmul(pb[:, m:m + 1], wst[:, k, m * P:(m + 1) * P],
                                                    lnb[:, k:k + 1], start=(k == 0), stop=(k == K - 1))
                    last.then_inc(s_bmp, 1)
                    norm_tensor(0, 0, 0)

        NW, NO, NV, NX, NG = 2, 2, 3, 2, 3
        NU = 3 * K + 4
        HALF = K // 2
        WR = sb("win_ring", [P, NW, XT, P])
        OR = sb("wout_ring", [P, NO, HALF, P])
        VS = sb("v_slots", [P, NV, ROWS + 2, PW])
        HA = sb("halo", [P, K, 2, W])
        UY = sb("uy", [P, NU, N])
        BB = sb("B_bc", [P, 2, NS, N])
        CB = sb("C_bc", [P, NS, N])
        XN = sb("xn", [P, XT, N + W])
        XR = sb("x_res", [P, NX, N])
        G = sb("g_ring", [P, NG, NS, N])
        EE = sb("sp_e", [P, N])
        LL = sb("sp_l", [P, N])
        RR = sb("sp_r", [P, 2, N])
        TM = sb("sp_t", [P, N])
        DU = sb("du", [P, N])
        SQ = sb("sq", [P, N])
        LS = sb("ln_sums", [P, N])
        MS = sb("ln_msq", [P, N])
        RS = sb("ln_rstd", [P, N])
        m1 = sb("minus_one", [P, 1])
        XD = sb("x_dbl", [64 + R, N])
        DA = sb("decay", [P, N])
        ST = sb("state", [P, K, NS])

        def ps(name, shape):
            return ctx.enter_context(nc.psum_tensor(name, shape, F32))

        p_in, p_cv, p_dt, p_ln, p_ms, p_op = (ps("p_" + n, [P, N]) for n in "in cv dt ln ms op".split())
        p_da = ps("p_da", [P, 2, N])
        decays = [p_da[:, 0, :], p_da[:, 1, :], DA[:]]
        NDA = len(decays)

        def sem(name):
            return ctx.enter_context(nc.semaphore(name))

        s_win = [sem(f"s_win{n}") for n in range(NW)]
        s_wor = [sem(f"s_wor{n}") for n in range(NO)]
        s_xin, s_bw, s_b, s_c = sem("s_xin"), sem("s_bw"), [sem("s_b0"), sem("s_b1")], sem("s_c")
        s_gv, s_gp, s_ga, s_st = sem("s_gv1"), sem("s_gp1"), sem("s_ga1"), sem("s_st1")
        s_xs = [sem(f"s_xst{n}") for n in range(4)]
        s_xrl = [sem(f"s_xrl{n}") for n in range(NX)]
        s_xrs = [sem(f"s_xrs{n}") for n in range(NX)]
        (s_xn, s_inp, s_row, s_rowev, s_vev, s_hin, s_hout, s_tap0, s_tap, s_silu, s_xp, s_xd, s_dt,
         s_abs, s_relu, s_e, s_l, s_w1, s_w3, s_delta, s_du, s_dbu, s_da, s_scan, s_scp, s_cm,
         s_ns1, s_ns2, s_y, s_sq, s_ln, s_ls, s_mean, s_msq, s_e2, s_var, s_vare, s_lv, s_rs0, s_nt,
         s_rstd, s_op, s_ov, s_bn, s_pad,
         s_zero, s_wp, s_wm, s_oa) = (sem("q_" + n) for n in (
             "xn inp row rowev vev hin hout tap0 tap silu xp xd dt abs relu e l w1 w3 delta du dbu da "
             "scan scp cm ns1 ns2 y sq ln ls mean msq e2 var vare lv rs0 nt rstd op ov bn pad "
             "zero wp wm oa").split())

        L_CONV, L_DT, L_SP, L_CH, L_SCAN, L_Y, L_SQ = 2, 14, 15, 16, 17, 18, 19
        S_XP, S_LN, S_OP = (9, 11, 14), 31, 31
        S_OV = S_OP + 2
        SLOTS = K * (NCH - 1) + S_OV + K + 1

        def tile(S, lag):
            i = S - lag
            return i if 0 <= i < NT else None

        def chunk_at(S, rel):
            c, r = divmod(S - rel, K)
            return c if r == 0 and 0 <= c < NCH else None

        def half_at(S):
            c, e = divmod(S - S_OP, K)
            return (c, *divmod(e, 2)) if 0 <= c < NCH else (None, None, None)

        def out_at(S, rel):
            r, odd = divmod(S - rel, 2)
            return r if not odd and 0 <= r < XT * NCH else None

        norm1_vector, norm1_tensor, norm1_scalar = group_norm_scale(
            nc.vector, nc.tensor, nc.scalar, nc, (s_gv, s_gp, s_ga), stats1[:, 1], CPB * XT, gtmp, p_op, quad[:],
            1e-5, gsc[:, 1:2], gbi[:, 1:2])
        NPIECE = CPB * XT
        S_NORM1 = NPIECE // 2 + 1

        def stage(n):
            return UY[:, NU - 4 + n % 4, :]

        def houts(i):
            if i < 0:
                return 0
            b, r = divmod(i, CPB * K)
            return b * (CPB - 1) * K + min(r + 1, (CPB - 1) * K)

        def hins(i):
            b, r = divmod(i, CPB * K)
            return b * (CPB - 1) * K + max(r - K + 1, 0)

        def zeros(i):
            b, r = divmod(i, CPB * K)
            return 2 * NV * b + min(r + 1, NV) + min(max(r + 1 - (CPB - 1) * K, 0), NV)

        def first_rows(i):
            b, r = divmod(i, CPB * K)
            return b * K + min(r + 1, K)

        def cols_of(c):
            k = c % CPB
            lo = 0 if k == 0 else (ROWS * k + 1) * W
            hi = T if k == CPB - 1 else (ROWS * (k + 1) + 1) * W
            return lo, hi

        def ucol(i):
            return UY[:, i % NU, :]

        TAPS = [(dy, dx) for dy in range(3) for dx in range(3) if (dy, dx) != (1, 1)]

        def win_view(i, dy, dx):
            return VS[:, i % NV, dy:dy + ROWS, dx:dx + W]

        def rows(ap):
            return ap.rearrange("p (r w) -> p r w", w=W)

        def load_x(eng, c):
            lo, hi = cols_of(c)
            wait(eng, s_inp, K * c)
            eng.dma_start(XN[:, :, 0:hi - lo], XTR[c // CPB, :, :, lo:hi]).then_inc(s_xin, 16)

        with nc.Block() as block:
            @block.sync
            def _(sp):
                def load_win(i):
                    if i < NT:
                        wait(sp, s_inp, i - NW + 1)
                        sp.dma_start(WR[:, i % NW], g["win"][i % K]).then_inc(s_win[i % NW], 16)

                def load_wout(e):
                    if e < 2 * XT * NCH:
                        wait(sp, s_op, e - NO + 1)
                        m, h = divmod(e % (2 * XT), 2)
                        sp.dma_start(OR[:, e % NO], woc_d[m, :, h * HALF:(h + 1) * HALF, :])\
                          .then_inc(s_wor[e % NO], 16)

                for i in range(NW - 1):
                    load_win(i)
                load_wout(0)
                for S in range(SLOTS):
                    if S == 0:
                        load_x(sp, 0)
                    load_win(S + NW - 1)
                    for n in (2 * S, 2 * S + 1):
                        if n < NPIECE:
                            t, k = divmod(n, CPB)
                            wait(sp, s_st, n - 3)
                            sp.dma_start(stage(n), XTR[1, :, t, k * N:(k + 1) * N]).then_inc(s_xs[n % 4], 16)
                    if S >= S_OP:
                        load_wout(S - S_OP + 1)
                    r = out_at(S, S_OV - 1)
                    if r is not None:
                        c, m = divmod(r, XT)
                        b, k = divmod(c, CPB)
                        if r >= NX:
                            sp.wait_ge(s_xrs[r % NX], 16 * (r // NX))
                            sp.wait_ge(s_bn, r - NX + 1)
                        sp.dma_start(XR[:, r % NX, :], XTR[b, :, m, k * N:(k + 1) * N])\
                          .then_inc(s_xrl[r % NX], 16)
                    r = out_at(S, S_OV + 2)
                    if r is not None:
                        c, m = divmod(r, XT)
                        b, k = divmod(c, CPB)
                        sp.wait_ge(s_ov, r + 1)
                        sp.dma_start(x1_d[b, :, m, k * N:(k + 1) * N], XR[:, r % NX, :])\
                          .then_inc(s_xrs[r % NX], 16)
                    if S % K == K - 1 and S < NT - 1:
                        load_x(sp, (S + 1) // K)
                    c = chunk_at(S, S_XP[2])
                    if c is not None:
                        sp.wait_ge(s_xd, c + 1)
                        sp.dma_start(bc_d[c], XD[R:R + 2 * NS, :]).then_inc(s_bw, 16)
                        sp.wait_ge(s_bw, 16 * (c + 1))
                        wait(sp, s_dbu, K * (c - 1))
                        sp.dma_start(BB[:, c % 2].rearrange("p n t -> p (n t)"),
                                     bc_d[c, 0:NS].rearrange("n t -> (n t)").partition_broadcast(P))\
                          .then_inc(s_b[c % 2], 16)
                    c = chunk_at(S, 16)
                    if c is not None:
                        wait(sp, s_cm, K * c)
                        sp.dma_start(CB[:].rearrange("p n t -> p (n t)"),
                                     bc_d[c, NS:2 * NS].rearrange("n t -> (n t)").partition_broadcast(P))\
                          .then_inc(s_c, 16)
                for n in range(NX):
                    sp.wait_ge(s_xrs[n], 16 * ((XT * NCH - n + NX - 1) // NX))

            @block.tensor
            def _(pe):
                def in_proj(i):
                    c, j = divmod(i, K)
                    lo, hi = cols_of(c)
                    pe.wait_ge(s_win[i % NW], 16 * (i // NW + 1))
                    pe.wait_ge(s_xn, c + 1)
                    wait(pe, s_vev, i)
                    wait(pe, s_hout, houts(i - 1))
                    off = 0
                    if c % CPB == 0:
                        off = W
                        for t in range(XT):
                            last = nc.tensor.matmul(p_in[:, 0:W], WR[:, i % NW, t, :], XN[:, t, 0:W],
                                                    start=(t == 0), stop=(t == XT - 1))
                        last.then_inc(s_row, 1)
                        pe.wait_ge(s_rowev, first_rows(i))
                    n = hi - lo - off
                    for t in range(XT):
                        last = nc.tensor.matmul(p_in[:, 0:n], WR[:, i % NW, t, :], XN[:, t, off:off + n],
                                                start=(t == 0), stop=(t == XT - 1))
                    last.then_inc(s_inp, 1)

                for S in range(SLOTS):
                    if S == S_NORM1:
                        norm1_tensor(0, 0, 0)
                    new = tile(S, 0)
                    if new is not None and S % K:
                        in_proj(new)
                    i = tile(S, L_SQ)
                    if i is not None:
                        c, j = divmod(i, K)
                        if j == 0:
                            wait(pe, s_ls, c)
                        q = j % 2
                        pe.wait_ge(s_y, i + 1)
                        nc.tensor.matmul(p_ln[64 + 32 * q:96 + 32 * q, :], ones32[:], ucol(i),
                                         start=(j < 2), stop=(j >= K - 2))
                        pe.wait_ge(s_sq, i + 1)
                        nc.tensor.matmul(p_ln[32 * q:32 * q + 32, :], ones32[:], SQ[:],
                                         start=(j < 2), stop=(j >= K - 2)).then_inc(s_ln, 1)
                    c = chunk_at(S, S_LN)
                    if c is not None:
                        pe.wait_ge(s_ls, c + 1)
                        wait(pe, s_xd, min(c + 2, NCH))
                        nc.tensor.matmul(p_ms[:], pick[:, 1, :], LS[:], start=True, stop=True).then_inc(s_mean, 1)
                    c, m, h = half_at(S)
                    if c is not None:
                        r = c * XT + m
                        e = 2 * r + h
                        if h == 0:
                            wait(pe, s_ov, r)
                        pe.wait_ge(s_wor[e % NO], 16 * (e // NO + 1))
                        for k in range(h * HALF, (h + 1) * HALF):
                            last = nc.tensor.matmul(p_op[:], OR[:, e % NO, k - h * HALF, :], ucol(c * K + k),
                                                    start=(k == 0), stop=(k == K - 1))
                        last.then_inc(s_op, 1)
                    c = chunk_at(S, S_LN)
                    if c is not None:
                        pe.wait_ge(s_msq, c + 1)
                        nc.tensor.matmul(p_ms[:], pick[:, 0, :], LS[:], start=True, stop=True).then_inc(s_e2, 1)
                    for q in range(3):
                        c = chunk_at(S, S_XP[q])
                        if c is None:
                            continue
                        pe.wait_ge(s_silu, 3 * c + q + 1)
                        wait(pe, s_var, c - 1)
                        for k in range(4 * q, 4 * q + 4):
                            last = nc.tensor.matmul(p_ms[0:R + 2 * NS, :], xpt[:, k, :], ucol(c * K + k),
                                                    start=(k == 0), stop=(k == K - 1))
                        if q == 2:
                            last.then_inc(s_xp, 1)
                    i = tile(S, L_DT)
                    if i is not None:
                        c, j = divmod(i, K)
                        pe.wait_ge(s_xd, c + 1)
                        wait(pe, s_relu, i)
                        h, jj = divmod(j, HALF)
                        nc.tensor.matmul(p_dt[:], dtt[64 * h:64 * h + R, jj * P:(jj + 1) * P],
                                         XD[64 * h:64 * h + R, :], start=True, stop=True).then_inc(s_dt, 1)
                    if new is not None and S % K == 0:
                        in_proj(new)

            @block.scalar
            def _(act):
                nc.scalar.preload_act_table_set(EXPSET)
                act.wait_ge(s_pad, 1)

                def load_norm(c):
                    lo, hi = cols_of(c)
                    act.wait_ge(s_xin, 16 * (c + 1))
                    b = c // CPB
                    o = XN[:, :, 0:hi - lo]
                    nc.scalar.activation(o, o, ACT.Identity, bias=gbi[:, b:b + 1], scale=gsc[:, b:b + 1])\
                      .then_inc(s_xn, 1)

                def decay(i, n):
                    j, e = i % K, NS * i + n
                    act.wait_ge(s_delta, i + 1)
                    wait(act, s_scan, e - NDA + 1)
                    nc.scalar.activation(decays[e % NDA], RR[:, i % 2, :], ACT.Exp,
                                         scale=At[:, j * NS + n:j * NS + n + 1]).then_inc(s_da, 1)

                def evacuate(i):
                    c, j = divmod(i, K)
                    k = c % CPB
                    wait(act, s_tap, len(TAPS) * (i - NV + 1))
                    if k > 0:
                        act.wait_ge(s_hout, houts(i - K))
                        nc.scalar.activation(VS[:, i % NV, 0:2, 1:1 + W], HA[:, j], ACT.Copy)\
                          .then_inc(s_hin, 1)
                    else:
                        act.wait_ge(s_row, first_rows(i))
                        nc.scalar.activation(VS[:, i % NV, 1, 1:1 + W], p_in[:, 0:W], ACT.Copy)\
                          .then_inc(s_rowev, 1)
                    act.wait_ge(s_inp, i + 1)
                    nr = ROWS - 1 if k == CPB - 1 else ROWS
                    nc.scalar.activation(VS[:, i % NV, 2:2 + nr, 1:1 + W], rows(p_in[:, 0:nr * W]), ACT.Copy)\
                      .then_inc(s_vev, 1)
                    if k < CPB - 1:
                        wait(act, s_hin, hins(i))
                        nc.scalar.activation(HA[:, j], rows(p_in[:, N - 2 * W:N]), ACT.Copy).then_inc(s_hout, 1)

                for S in range(SLOTS):
                    if S == S_NORM1:
                        norm1_scalar(0, 0, 0)
                    i = tile(S, L_SCAN)
                    if i is not None:
                        decay(i, NS - 1)
                    i = tile(S, L_SQ)
                    if i is not None:
                        act.wait_ge(s_y, i + 1)
                        wait(act, s_ln, i)
                        nc.scalar.activation(SQ[:], ucol(i), ACT.Square).then_inc(s_sq, 1)
                    c = chunk_at(S, S_LN + 1)
                    if c is not None:
                        act.wait_ge(s_vare, c + 1)
                        wait(act, s_ov, XT * c)
                        nc.scalar.activation(RS[:], MS[:], ACT.Ln).then_inc(s_lv, 1)
                        act.wait_ge(s_lv, c + 1)
                        nc.scalar.activation(RS[:], RS[:], ACT.Exp, scale=-0.5).then_inc(s_rs0, 1)
                    i = tile(S, L_SP)
                    if i is not None:
                        j, h = i % K, i % 2
                        act.wait_ge(s_dt, i + 1)
                        wait(act, s_delta, i)
                        nc.scalar.activation(EE[:], p_dt[:], ACT.Abs, bias=dtb[:, j:j + 1]).then_inc(s_abs, 1)
                        wait(act, s_dbu, i - 1)
                        wait(act, s_da, NS * (i - 1))
                        nc.scalar.activation(RR[:, h, :], p_dt[:], ACT.Relu, bias=dtb[:, j:j + 1]).then_inc(s_relu, 1)
                        act.wait_ge(s_abs, i + 1)
                        nc.scalar.activation(EE[:], EE[:], ACT.Exp, scale=-1.0).then_inc(s_e, 1)
                        act.wait_ge(s_e, i + 1)
                        nc.scalar.activation(LL[:], EE[:], ACT.Identity, bias=1.0).then_inc(s_wp, 1)
                        act.wait_ge(s_wp, i + 1)
                        nc.scalar.activation(TM[:], LL[:], ACT.Identity, bias=m1[:]).then_inc(s_wm, 1)
                        act.wait_ge(s_wm, i + 1)
                        nc.scalar.activation(LL[:], LL[:], ACT.Ln).then_inc(s_l, 1)
                    if S % K == 0 and S < NT:
                        load_norm(S // K)
                    new = tile(S, 0)
                    if new is not None and S % K:
                        evacuate(new)
                    if S >= 6 and S % 4 == 2 and (S - 6) // 4 < NT // 4:
                        q = (S - 6) // 4
                        act.wait_ge(s_tap, len(TAPS) * 4 * (q + 1))
                        o = UY[:, 4 * q % NU:4 * q % NU + 4, :]
                        nc.scalar.activation(o, o, ACT.Silu).then_inc(s_silu, 1)
                        nc.scalar.preload_act_table_set(EXPSET)
                    c = chunk_at(S, S_LN)
                    if c is not None:
                        act.wait_ge(s_mean, c + 1)
                        nc.scalar.activation(MS[:], p_ms[:], ACT.Square).then_inc(s_msq, 1)
                    c = chunk_at(S, S_LN - 1)
                    if c is not None:
                        act.wait_ge(s_ln, K * (c + 1))
                        nc.scalar.activation(LS[:], p_ln[:], ACT.Copy).then_inc(s_ls, 1)
                    i = tile(S, L_CONV - 1)
                    if i is not None:
                        j = i % K
                        act.wait_ge(s_vev, i + 1)
                        wait(act, s_hin, hins(i))
                        wait(act, s_zero, zeros(i))
                        wait(act, s_rowev, first_rows(i))
                        wait(act, s_tap, len(TAPS) * i)
                        nc.scalar.activation(rows(p_cv[:]), win_view(i, 1, 1), ACT.Identity,
                                             bias=convb[:, j:j + 1], scale=cwt[:, j, 4:5]).then_inc(s_tap0, 1)
                    i = tile(S, L_CH)
                    if i is not None:
                        for n in range(NS - 1):
                            decay(i, n)
                    c = chunk_at(S, S_XP[2])
                    if c is not None:
                        act.wait_ge(s_xp, c + 1)
                        wait(act, s_dt, K * c)
                        wait(act, s_bw, 16 * c)
                        nc.scalar.activation(XD[0:R + 2 * NS, :], p_ms[0:R + 2 * NS, :], ACT.Copy)
                        nc.scalar.activation(XD[64:64 + R, :], p_ms[0:R, :], ACT.Copy).then_inc(s_xd, 1)
                    if new is not None and S % K == 0:
                        evacuate(new)

            @block.gpsimd
            def _(pool):
                nc.gpsimd.memset(m1[:], -1.0)
                nc.gpsimd.memset(VS[:], 0.0).then_inc(s_pad, 1)
                pool.wait_ge(s_pad, 1)
                for S in range(SLOTS):
                    i = tile(S, L_CH)
                    if i is not None:
                        h = i % 2
                        pool.wait_ge(s_l, i + 1)
                        nc.gpsimd.tensor_tensor(TM[:], EE[:], TM[:], ALU.subtract).then_inc(s_w1, 1)
                        nc.gpsimd.tensor_tensor(RR[:, h, :], RR[:, h, :], LL[:], ALU.add).then_inc(s_w3, 1)
                        pool.wait_ge(s_w1, i + 1)
                        pool.wait_ge(s_w3, i + 1)
                        nc.gpsimd.tensor_tensor(RR[:, h, :], RR[:, h, :], TM[:], ALU.add).then_inc(s_delta, 1)
                    i = tile(S, L_Y)
                    if i is not None:
                        gi = G[:, i % NG]
                        pool.wait_ge(s_cm, i + 1)
                        nc.gpsimd.tensor_tensor(gi[:, 0:2], gi[:, 0:2], gi[:, 2:4], ALU.add).then_inc(s_ns1, 1)
                    i = tile(S, L_CH)
                    if i is not None:
                        c, j = divmod(i, K)
                        h = i % 2
                        pool.wait_ge(s_delta, i + 1)
                        wait(pool, s_dbu, i)
                        nc.gpsimd.tensor_tensor(DU[:], RR[:, h, :], ucol(i), ALU.mult).then_inc(s_du, 1)
                        pool.wait_ge(s_du, i + 1)
                        wait(pool, s_y, i - NG + 1)
                        pool.wait_ge(s_b[c % 2], 16 * (c // 2 + 1))
                        nc.gpsimd.tensor_tensor(G[:, i % NG], DU[:].unsqueeze(1).broadcast_to([P, NS, N]),
                                                BB[:, c % 2], ALU.mult).then_inc(s_dbu, 1)
                    i = tile(S, 0)
                    if i is not None:
                        k, j = (i // K) % CPB, i % K
                        if j < NV and k in (0, CPB - 1):
                            wait(pool, s_tap, len(TAPS) * (i - NV + 1))
                            nc.gpsimd.memset(VS[:, i % NV, 0 if k == 0 else ROWS + 1, :], 0.0).then_inc(s_zero, 1)

            @block.vector
            def _(vec):
                def scan(i, n):
                    c, j = divmod(i, K)
                    e = NS * i + n
                    vec.wait_ge(s_dbu, i + 1)
                    vec.wait_ge(s_da, e + 1)
                    init = 0.0
                    if c % CPB:
                        vec.wait_ge(s_scp, i - K + 1)
                        init = ST[:, j, n:n + 1]
                    gn = G[:, i % NG, n, :]
                    nc.vector.tensor_tensor_scan(gn, decays[e % NDA], gn, init, ALU.mult, ALU.add)\
                      .then_inc(s_scan, 1)

                def keep_state(i):
                    vec.wait_ge(s_scan, NS * (i + 1))
                    nc.vector.tensor_copy(ST[:, i % K, :], G[:, i % NG, :, N - 1]).then_inc(s_scp, 1)

                def times_c(i):
                    vec.wait_ge(s_scp, i + 1)
                    vec.wait_ge(s_c, 16 * (i // K + 1))
                    gi = G[:, i % NG]
                    nc.vector.tensor_tensor(gi, gi, CB[:], ALU.mult).then_inc(s_cm, 1)

                def tap(i, q):
                    dy, dx = TAPS[q]
                    c, j = divmod(i, K)
                    if q == 0:
                        vec.wait_ge(s_tap0, i + 1)
                    else:
                        vec.wait_ge(s_tap, len(TAPS) * i + q)
                    dst = p_cv[:]
                    if q == len(TAPS) - 1:
                        dst = ucol(i)
                        if i >= NU:
                            cf, jf = divmod(i - NU, K)
                            vec.wait_ge(s_op, 2 * XT * cf + 2 * XT - (1 if jf < HALF else 0))
                    nc.vector.scalar_tensor_tensor(rows(dst), win_view(i, dy, dx),
                                                   cwt[:, j, 3 * dy + dx:3 * dy + dx + 1],
                                                   rows(p_cv[:]), ALU.mult, ALU.add).then_inc(s_tap, 1)

                def skip_add(i):
                    vec.wait_ge(s_ns1, i + 1)
                    vec.wait_ge(s_du, i + 1)
                    nc.vector.scalar_tensor_tensor(ucol(i), ucol(i), Dp[:, i % K:i % K + 1], G[:, i % NG, 0, :],
                                                   ALU.mult, ALU.add).then_inc(s_ns2, 1)

                def last_add(i):
                    vec.wait_ge(s_ns2, i + 1)
                    nc.vector.tensor_tensor(ucol(i), ucol(i), G[:, i % NG, 1, :], ALU.add).then_inc(s_y, 1)

                def scale_out(r):
                    vec.wait_ge(s_op, 2 * r + 2)
                    vec.wait_ge(s_rstd, r // XT + 1)
                    nc.vector.tensor_tensor(p_op[:], p_op[:], RS[:], ALU.mult).then_inc(s_oa, 1)

                def residual_add(r):
                    m = r % XT
                    vec.wait_ge(s_oa, r + 1)
                    vec.wait_ge(s_xrl[r % NX], 16 * (r // NX + 1))
                    nc.vector.scalar_tensor_tensor(XR[:, r % NX, :], p_op[:], bm[:, m:m + 1], XR[:, r % NX, :],
                                                   ALU.add, ALU.add).then_inc(s_ov, 1)

                for S in range(SLOTS):
                    for n in (2 * S - 2, 2 * S - 1):
                        if 0 <= n < NPIECE:
                            vec.wait_ge(s_xs[n % 4], 16 * (n // 4 + 1))
                            nc.vector.bn_stats(stats1[:, 1, n, :], stage(n)).then_inc(s_st, 1)
                    if S == S_NORM1:
                        vec.wait_ge(s_st, NPIECE)
                        norm1_vector(0, 0, 0)
                    a, b, y, r = tile(S, L_SCAN), tile(S, L_CONV), tile(S, L_Y), out_at(S, S_OV)
                    c = chunk_at(S, S_LN + 1)
                    if c is not None:
                        vec.wait_ge(s_e2, c + 1)
                        nc.vector.tensor_tensor(MS[:], p_ms[:], MS[:], ALU.subtract).then_inc(s_var, 1)
                        vec.wait_ge(s_var, c + 1)
                        nc.vector.tensor_scalar(MS[:], MS[:], 0.0, 1e-5, ALU.max, ALU.add).then_inc(s_vare, 1)
                    for n in range(NS):
                        if a is not None:
                            scan(a, n)
                        if b is not None:
                            tap(b, n)
                        if n == 0 and r is not None:
                            scale_out(r)
                        if n == 1 and r is not None:
                            residual_add(r)
                    if a is not None:
                        keep_state(a)
                    if b is not None:
                        tap(b, 4)
                    if b is not None:
                        for n in range(5, len(TAPS)):
                            tap(b, n)
                    if a is not None:
                        times_c(a)
                    c = chunk_at(S, S_LN + 1)
                    if c is not None:
                        vec.wait_ge(s_rs0, c + 1)
                        nc.vector.tensor_tensor(LS[:], RS[:], RS[:], ALU.mult).then_inc(s_nt, 1)
                        vec.wait_ge(s_nt, 3 * c + 1)
                        nc.vector.tensor_tensor(LS[:], LS[:], MS[:], ALU.mult).then_inc(s_nt, 1)
                        vec.wait_ge(s_nt, 3 * c + 2)
                        nc.vector.tensor_scalar(LS[:], LS[:], -0.5, 1.5, ALU.mult, ALU.add).then_inc(s_nt, 1)
                        vec.wait_ge(s_nt, 3 * c + 3)
                        nc.vector.tensor_tensor(RS[:], RS[:], LS[:], ALU.mult).then_inc(s_rstd, 1)
                    if y is not None:
                        skip_add(y)
                        last_add(y)
                    r = out_at(S, S_OV + 1)
                    if r is not None:
                        c, m = divmod(r, XT)
                        bb, k = divmod(c, CPB)
                        vec.wait_ge(s_ov, r + 1)
                        nc.vector.bn_stats(stats1[:, bb, m * CPB + k, :], XR[:, r % NX, :]).then_inc(s_bn, 1)


def layer1(nc, g):
    (B, C, T, N, CPB, XT) = (g[n] for n in "B C T N CPB XT".split())
    x1_d, ws_d, OUTR = g["x1_d"], g["ws_d"], g["OUTR"]
    quad, gsc, gbi, stats1, gtmp = g["quad"], g["gsc"], g["gbi"], g["stats1"], g["gtmp"]
    NH = 12
    TB = N // P
    NR = 4
    with ExitStack() as ctx:
        def sb(name, shape, dtype=F32):
            return ctx.enter_context(nc.sbuf_tensor(name, shape, dtype))

        WX = sb("w_split", [P, XT, 2, C], F32R)
        WS = sb("wo_split", [P, 2, C], F32R)
        WR = sb("wo_raw", [P, C])
        XH = sb("x_split", [P, NR, 2, N], F32R)
        XC = sb("xc", [P, 2, XT, N])
        WW = sb("w_all", [P, XT, T])
        JK = sb("junk", [P, 2, N])
        n2 = sb("n2", [P, XT, CPB])
        dn = sb("dn", [P, XT, CPB])
        small = sb("small", [P, 8, XT])
        tmpc = sb("tmpc", [P, XT])
        sel = sb("sel", [P, XT, NH])
        lsel = sb("lsel", [P, XT, NH])
        selb = sb("selb", [NH, C], F32R)
        ident = sb("ident", [P, P])
        mx = sb("mx", [P, 4, TB])
        lz = sb("lz", [P, TB, NH])
        pi = sb("pi", [P, TB, NH])
        LT = sb("logits_t", [NH, N])
        PT = sb("pi_t", [NH, 2, 2, N], F32R)
        sh = sb("sh", [NH, CPB + 1])

        banks = ctx.enter_context(nc.psum_tensor("banks", [P, 8, N], F32))
        p_w, p_pb = banks[:, 0:XT, :], banks[:, 0:2, :]
        p_lt, p_lg = banks[:, 6, :], banks[:, 5, :]
        p_pt = banks[:, 7, :]
        p_sm, p_sh = banks[:, 7, :], banks[:, 4, :]

        def sem(name):
            return ctx.enter_context(nc.semaphore(name))

        s_par, s_gv, s_gp, s_ga = sem("t_par"), sem("t_gv"), sem("t_gp"), sem("t_ga")
        s_xl = [sem("t_xl0"), sem("t_xl1")]
        s_os = [sem("t_os0"), sem("t_os1")]
        s_wx = [sem(f"t_wx{q}") for q in range(XT)]
        (s_wq, s_wh, s_wl, s_wor, s_oh, s_ol, s_wos, s_wqs, s_hi, s_lo, s_mm, s_acc, s_ev,
         s_xn, s_ss, s_n2, s_lsel, s_w2, s_lg, s_mx, s_lz, s_ez, s_pi, s_tp, s_pt, s_pb, s_q,
         s_dn, s_sp, s_fin, s_sh, s_lt, s_tl, s_sum, s_pl, s_qc, s_sel) = (sem("t_" + n) for n in (
             "wq wh wl wor oh ol wos wqs hi lo mm acc ev "
             "xn ss n2 lsel w2 lg mx lz ez pi tp pt pb q dn sp fin sh lt tl sum pl qc sel").split())
        params = [(tmpc[:], g["temp"]), (sel[:], g["sel_d"]), (ident[:], g["ident_d"]),
                  (JK[0:NH].rearrange("p s n -> p (s n)")[:, 0:C], g["selb_d"])]
        NP_ = 16 * len(params)
        NM, NF = 3, 6

        def steps(b):
            return group_norm_scale(nc.vector, nc.tensor, nc.scalar, nc, (s_gv, s_gp, s_ga),
                                    stats1[:, b], CPB * XT, gtmp, p_sm, quad[:], 1e-5,
                                    gsc[:, B + b:B + b + 1], gbi[:, B + b:B + b + 1])

        def wait_used(eng, h):
            if h >= 0:
                u, q = divmod(h, XT)
                if q == XT - 1:
                    eng.wait_ge(s_acc, XT * (u + 1))
                else:
                    eng.wait_ge(s_mm, (XT - 1) * u + q + 1)

        def hi(h):
            return XH[:, h % NR, 0, :]

        def lo(h):
            return XH[:, h % NR, 1, :]

        def f32(ap):
            return ap.bitcast(F32)

        with nc.Block() as block:
            @block.sync
            def _(sp):
                def store(b, k):
                    u = (2 * b + 1) * CPB + k
                    sp.wait_ge(s_ev, XT * (u + 1))
                    sp.dma_start(OUTR[b, :, :, k * N:(k + 1) * N], XC[:, k % 2]).then_inc(s_os[k % 2], 16)

                def load_weights(b, ph):
                    for q in range(XT):
                        wait_used(sp, XT * ((2 * b + ph) * CPB - 1) + q)
                        sp.dma_start(f32(WX[:, q]), ws_d[ph, q]).then_inc(s_wx[q], 16)

                sp.dma_start(WW[:, :, 0:C], g["wqkv"]).then_inc(s_wq, 16)
                for dst, src in params:
                    sp.dma_start(dst, src).then_inc(s_par, 16)
                def load_x(b, k):
                    u = 2 * b * CPB + k
                    if k >= 2:
                        sp.wait_ge(s_lo, XT * (u - 1))
                    elif b:
                        sp.wait_ge(s_os[k], 16 * (b * CPB // 2))
                    sp.dma_start(XC[:, u % 2], x1_d[b, :, :, k * N:(k + 1) * N]).then_inc(s_xl[u % 2], 16)

                for b in range(B):
                    for k in range(CPB):
                        if b == 0 or k > 0:
                            load_x(b, k)
                        if b == 0:
                            q = k - 1
                            if k == 1:
                                sp.wait_ge(s_wh, XT)
                                sp.wait_ge(s_wl, XT)
                                for q2 in range(XT):
                                    sp.dma_start(ws_d[0, q2], f32(WX[:, q2])).then_inc(s_wqs, 16)
                            if 0 <= q < XT:
                                wait(sp, s_oh, q)
                                wait(sp, s_ol, q)
                                sp.dma_start(WR[:], g["wo2"][:, q, :]).then_inc(s_wor, 16)
                            if 0 < q <= XT:
                                sp.wait_ge(s_oh, q)
                                sp.wait_ge(s_ol, q)
                                sp.dma_start(ws_d[1, q - 1], f32(WS[:])).then_inc(s_wos, 16)
                    if b == 0:
                        sp.wait_ge(s_wqs, 16 * XT)
                        sp.wait_ge(s_wos, 16 * XT)
                    load_weights(b, 1)
                    for k in range(CPB):
                        u = (2 * b + 1) * CPB + k
                        if k < 2:
                            sp.wait_ge(s_lg, b * CPB + CPB - 1 + k)
                        else:
                            sp.wait_ge(s_os[u % 2], 16 * ((b * CPB + k - 2) // 2 + 1))
                        sp.dma_start(XC[:, u % 2], x1_d[b, :, :, k * N:(k + 1) * N]).then_inc(s_xl[u % 2], 16)
                        if k >= 1:
                            store(b, k - 1)
                    if b < B - 1:
                        load_x(b + 1, 0)
                        load_weights(b + 1, 0)
                    store(b, CPB - 1)
                for n in range(2):
                    sp.wait_ge(s_os[n], 16 * (B * CPB // 2))

            @block.tensor
            def _(pe):
                def product(b, ph, k):
                    u = (2 * b + ph) * CPB + k
                    for q in range(XT):
                        h = XT * u + q
                        if u == 0:
                            pe.wait_ge(s_wl, q + 1)
                        elif k == 0:
                            pe.wait_ge(s_wx[q], 16 * (2 * b + ph))
                        pe.wait_ge(s_lo, h + 1)
                        for m in range(XT):
                            if q == 0:
                                wait(pe, s_ev, XT * (u - 1) + m + 1)
                            cols = slice(m * P, (m + 1) * P)
                            nc.tensor.matmul(p_w[:, m, :], WX[:, q, 0, cols], hi(h), start=(q == 0), stop=False)
                            nc.tensor.matmul(p_w[:, m, :], WX[:, q, 0, cols], lo(h), start=False, stop=False)
                            last = nc.tensor.matmul(p_w[:, m, :], WX[:, q, 1, cols], hi(h),
                                                    start=False, stop=(q == XT - 1))
                            if q == XT - 1:
                                last.then_inc(s_acc, 1)
                        if q < XT - 1:
                            last.then_inc(s_mm, 1)

                for b in range(B):
                    steps(b)[1](b * GN_V, b * GN_P, b * GN_A)
                pe.wait_ge(s_par, NP_)
                for b in range(B):
                    for k in range(CPB):
                        product(b, 0, k)
                    pe.wait_ge(s_lsel, b + 1)

                    def logits(k, tiles):
                        if k >= CPB:
                            return
                        cc = b * CPB + k
                        for t in tiles:
                            pe.wait_ge(s_w2, XT * cc + t + 1)
                            wait(pe, s_lt, cc)
                            last = nc.tensor.matmul(p_lt[0:NH, :], lsel[:, t, :], XC[:, k % 2, t, :],
                                                    start=(t == 0), stop=(t == XT - 1))
                            if t == XT - 1:
                                last.then_inc(s_lg, 1)

                    def broadcast(k, t):
                        if k < 0:
                            return
                        cc = b * CPB + k
                        n = XT * cc + t
                        pe.wait_ge(s_pl, cc + 1)
                        wait(pe, s_q, n - 1)
                        cols = slice(t * P, (t + 1) * P)
                        nc.tensor.matmul(p_pb[:, n % 2, :], selb[:, cols], PT[:, k % 2, 0, :], start=True, stop=False)
                        nc.tensor.matmul(p_pb[:, n % 2, :], selb[:, cols], PT[:, k % 2, 1, :], start=False, stop=True)\
                          .then_inc(s_pb, 1)

                    for k in range(-2, CPB):
                        cc = b * CPB + k
                        softmax = 0 <= k + 1 < CPB
                        broadcast(k, 0)
                        broadcast(k, 1)
                        if softmax:
                            pe.wait_ge(s_lt, cc + 2)
                            wait(pe, s_lz, cc + 1)
                            for tb in range(TB):
                                last = nc.tensor.transpose(p_lg[:, tb * NH:(tb + 1) * NH],
                                                           LT[:, tb * P:(tb + 1) * P], ident[0:NH, 0:NH])
                            last.then_inc(s_tl, 1)
                        logits(k + 2, (0, 1))
                        broadcast(k, 2)
                        logits(k + 2, (2, 3))
                        broadcast(k, 3)
                        logits(k + 2, (4, 5))
                        broadcast(k, 4)
                        if softmax:
                            pe.wait_ge(s_pi, cc + 2)
                            wait(pe, s_pl, cc + 1)
                            for tb in range(TB):
                                last = nc.tensor.transpose(p_pt[0:NH, tb * P:(tb + 1) * P], pi[:, tb, :], ident[:])
                            last.then_inc(s_tp, 1)
                        broadcast(k, 5)
                    pe.wait_ge(s_sh, b + 1)
                    for t in range(XT):
                        last = nc.tensor.matmul(p_sh[:, t:t + 1], f32(selb[:, t * P:(t + 1) * P]),
                                                sh[:, CPB:CPB + 1], start=True, stop=True)
                    last.then_inc(s_sp, 1)
                    for k in range(CPB):
                        product(b, 1, k)

            @block.scalar
            def _(act):
                nc.scalar.preload_act_table_set(EXPSET)
                act.wait_ge(s_wq, 16)
                for q in range(XT):
                    nc.scalar.activation(WX[:, q, 0, :], WW[:, q, 0:C], ACT.Copy).then_inc(s_wh, 1)
                act.wait_ge(s_par, NP_)
                nc.scalar.activation(selb[:], JK[0:NH].rearrange("p s n -> p (s n)")[:, 0:C], ACT.Copy)\
                  .then_inc(s_sel, 1)
                act.wait_ge(s_sel, 1)
                for b in range(B):
                    steps(b)[2](b * GN_V, b * GN_P, b * GN_A)
                for b in range(B):
                    act.wait_ge(s_gv, GN_V * B)

                    def squares(k, t):
                        n = XT * (b * CPB + k) + t
                        act.wait_ge(s_ev, XT * (2 * b * CPB + k) + t + 1)
                        wait(act, s_ss, n - 1)
                        nc.scalar.activation(JK[:, n % 2, :], WW[:, t, k * N:(k + 1) * N], ACT.Square,
                                             accum_out=n2[:, t, k:k + 1]).then_inc(s_ss, 1)

                    for k in range(CPB):
                        cc = b * CPB + k
                        u = 2 * b * CPB + k
                        act.wait_ge(s_xl[u % 2], 16 * (u // 2 + 1))
                        o = XC[:, u % 2]
                        nc.scalar.activation(o, o, ACT.Identity, bias=gbi[:, B + b:B + b + 1],
                                             scale=gsc[:, B + b:B + b + 1]).then_inc(s_xn, 1)
                        act.wait_ge(s_xn, cc + 1)

                        def round_x(t):
                            wait_used(act, XT * u + t - NR)
                            nc.scalar.activation(hi(XT * u + t), XC[:, u % 2, t, :], ACT.Copy).then_inc(s_hi, 1)

                        for t in range(NR - 1):
                            round_x(t)
                        for t in range(XT):
                            if k >= 1:
                                squares(k - 1, t)
                            if NR - 2 <= t < XT - 1:
                                round_x(t + 1)
                        if b == 0 and 1 <= k <= XT:
                            act.wait_ge(s_wor, 16 * k)
                            wait(act, s_wos, 16 * (k - 1))
                            nc.scalar.activation(WS[:, 0, :], WR[:], ACT.Copy).then_inc(s_oh, 1)
                    for t in range(XT):
                        squares(CPB - 1, t)
                    act.wait_ge(s_lo, XT * (2 * b + 1) * CPB)

                    def square_w(k, tiles):
                        if k >= CPB:
                            return
                        wait(act, s_lg, b * CPB + k - 1)
                        for t in tiles:
                            nc.scalar.activation(XC[:, k % 2, t, :], WW[:, t, k * N:(k + 1) * N], ACT.Square)\
                              .then_inc(s_w2, 1)

                    def keep_q(k, t):
                        if k >= 0:
                            n = XT * (b * CPB + k) + t
                            act.wait_ge(s_dn, n + 1)
                            nc.scalar.activation(WW[:, t, k * N:(k + 1) * N], JK[:, n % 2, :], ACT.Copy)\
                              .then_inc(s_qc, 1)

                    for k in range(-3, CPB):
                        cc = b * CPB + k
                        softmax = 0 <= k + 1 < CPB
                        keep_q(k, 0)
                        keep_q(k, 1)
                        if softmax:
                            act.wait_ge(s_lz, cc + 2)
                            nc.scalar.activation(lz[:], lz[:], ACT.Exp).then_inc(s_ez, 1)
                        square_w(k + 3, (0, 1))
                        keep_q(k, 2)
                        square_w(k + 3, (2, 3))
                        keep_q(k, 3)
                        if softmax:
                            act.wait_ge(s_tp, cc + 2)
                            nc.scalar.activation(LT[:], p_pt[0:NH, :], ACT.Copy, accum_out=sh[:, k + 1:k + 2])\
                              .then_inc(s_sum, 1)
                            wait(act, s_pb, XT * cc)
                            nc.scalar.activation(PT[:, (k + 1) % 2, 0, :], p_pt[0:NH, :], ACT.Copy).then_inc(s_pt, 1)
                        square_w(k + 3, (4, 5))
                        if 0 <= k + 2 < CPB:
                            act.wait_ge(s_lg, cc + 3)
                            wait(act, s_pt, cc + 2)
                            nc.scalar.activation(LT[:], p_lt[0:NH, :], ACT.Copy).then_inc(s_lt, 1)
                        keep_q(k, 4)
                        keep_q(k, 5)
                    act.wait_ge(s_fin, NF * (b + 1))
                    act.wait_ge(s_qc, XT * CPB * (b + 1))
                    for k in range(CPB):
                        u = (2 * b + 1) * CPB + k
                        for t in range(XT):
                            wait_used(act, XT * u + t - NR)
                            nc.scalar.activation(hi(XT * u + t), WW[:, t, k * N:(k + 1) * N], ACT.Copy,
                                                 scale=small[:, 5, t:t + 1]).then_inc(s_hi, 1)

            @block.vector
            def _(vec):
                vec.wait_ge(s_wq, 16)
                for q in range(XT):
                    vec.wait_ge(s_wh, q + 1)
                    nc.vector.tensor_sub(WX[:, q, 1, :], WW[:, q, 0:C], f32(WX[:, q, 0, :])).then_inc(s_wl, 1)
                for b in range(B):
                    wait(vec, s_gv, GN_V * b)
                    steps(b)[0](b * GN_V, b * GN_P, b * GN_A)
                vec.wait_ge(s_par, NP_)
                for b in range(B):
                    def keep_w(k, t):
                        n = XT * (2 * b * CPB + k) + t
                        vec.wait_ge(s_acc, n + 1)
                        if n == 0:
                            vec.wait_ge(s_wl, XT)
                        nc.vector.tensor_copy(WW[:, t, k * N:(k + 1) * N], p_w[:, t, :]).then_inc(s_ev, 1)

                    def rest_of_x(k, t):
                        h = XT * (2 * b * CPB + k) + t
                        vec.wait_ge(s_hi, h + 1)
                        nc.vector.tensor_sub(lo(h), XC[:, k % 2, t, :], f32(hi(h))).then_inc(s_lo, 1)

                    for k in range(CPB):
                        for t in range(NR - 1):
                            rest_of_x(k, t)
                        if k:
                            for t in range(XT):
                                keep_w(k - 1, t)
                        for t in range(NR - 1, XT):
                            rest_of_x(k, t)
                        if b == 0 and 1 <= k <= XT:
                            vec.wait_ge(s_oh, k)
                            nc.vector.tensor_sub(WS[:, 1, :], WR[:], f32(WS[:, 0, :])).then_inc(s_ol, 1)
                    for t in range(XT):
                        keep_w(CPB - 1, t)
                    vec.wait_ge(s_ss, XT * CPB * (b + 1))
                    nc.vector.reduce_sum(small[:, 0, :], n2[:], AX.X).then_inc(s_n2, 1)
                    vec.wait_ge(s_n2, 4 * b + 1)
                    nc.vector.tensor_scalar(small[:, 0, :], small[:, 0, :], 1e-24, None, ALU.max).then_inc(s_n2, 1)
                    vec.wait_ge(s_n2, 4 * b + 2)
                    nc.vector.reciprocal(small[:, 1, :], small[:, 0, :]).then_inc(s_n2, 1)
                    vec.wait_ge(s_n2, 4 * b + 3)
                    nc.vector.tensor_mul(small[:, 6, :], small[:, 1, :], tmpc[:]).then_inc(s_n2, 1)
                    vec.wait_ge(s_n2, 4 * b + 4)
                    wait(vec, s_lg, CPB * b)
                    nc.vector.tensor_tensor(lsel[:], sel[:], small[:, 6, :].unsqueeze(2).broadcast_to([P, XT, NH]),
                                            ALU.mult).then_inc(s_lsel, 1)
                    lg = p_lg[:, 0:TB * NH].rearrange("p (t h) -> p t h", h=NH)

                    def less_max(cc):
                        vec.wait_ge(s_tl, cc + 1)
                        nc.vector.tensor_reduce(mx[:, 0, :], lg, AX.X, ALU.max).then_inc(s_mx, 1)
                        vec.wait_ge(s_mx, NM * cc + 1)
                        wait(vec, s_pi, cc)
                        nc.vector.tensor_tensor(lz[:], lg, mx[:, 0, :].unsqueeze(2).broadcast_to([P, TB, NH]),
                                                ALU.subtract).then_inc(s_lz, 1)

                    def over_sum(cc):
                        vec.wait_ge(s_ez, cc + 1)
                        nc.vector.reduce_sum(mx[:, 1, :], lz[:], AX.X).then_inc(s_mx, 1)
                        vec.wait_ge(s_mx, NM * cc + 2)
                        nc.vector.reciprocal(mx[:, 2, :], mx[:, 1, :]).then_inc(s_mx, 1)
                        vec.wait_ge(s_mx, NM * cc + 3)
                        wait(vec, s_tp, cc)
                        nc.vector.tensor_tensor(pi[:], lz[:], mx[:, 2, :].unsqueeze(2).broadcast_to([P, TB, NH]),
                                                ALU.mult).then_inc(s_pi, 1)

                    def weigh(k, t):
                        if k < 0:
                            return
                        n = XT * (b * CPB + k) + t
                        o = WW[:, t, k * N:(k + 1) * N]
                        vec.wait_ge(s_pb, n + 1)
                        wait(vec, s_qc, n - 1)
                        nc.vector.tensor_tensor(JK[:, n % 2, :], o, p_pb[:, n % 2, :], ALU.mult).then_inc(s_q, 1)
                        vec.wait_ge(s_q, n + 1)
                        nc.vector.tensor_tensor_reduce(out=o, in0=o, in1=JK[:, n % 2, :], scale=1.0, scalar=0.0,
                                                       op0=ALU.mult, op1=ALU.add,
                                                       accum_out=dn[:, t, k:k + 1]).then_inc(s_dn, 1)

                    for k in range(-1, CPB):
                        cc = b * CPB + k
                        more = k + 1 < CPB
                        weigh(k, 0)
                        weigh(k, 1)
                        if more:
                            less_max(cc + 1)
                        weigh(k, 2)
                        weigh(k, 3)
                        if more:
                            over_sum(cc + 1)
                        weigh(k, 4)
                        if more:
                            vec.wait_ge(s_pt, cc + 2)
                            nc.vector.tensor_sub(PT[:, (k + 1) % 2, 1, :], p_pt[0:NH, :],
                                                 f32(PT[:, (k + 1) % 2, 0, :])).then_inc(s_pl, 1)
                        weigh(k, 5)
                    vec.wait_ge(s_pt, CPB * (b + 1))
                    nc.vector.reduce_sum(sh[:, CPB:CPB + 1], sh[:, 0:CPB], AX.X).then_inc(s_sh, 1)
                    f0 = NF * b
                    vec.wait_ge(s_dn, XT * CPB * (b + 1))
                    nc.vector.reduce_sum(small[:, 2, :], dn[:], AX.X).then_inc(s_fin, 1)
                    vec.wait_ge(s_sp, b + 1)
                    nc.vector.tensor_scalar(small[:, 3, :], p_sh[:, 0:XT], 1e-8, None, ALU.add)\
                      .then_inc(s_fin, 1)
                    vec.wait_ge(s_fin, f0 + 2)
                    nc.vector.reciprocal(small[:, 4, :], small[:, 3, :]).then_inc(s_fin, 1)
                    vec.wait_ge(s_fin, f0 + 3)
                    nc.vector.tensor_mul(small[:, 2, :], small[:, 2, :], small[:, 4, :]).then_inc(s_fin, 1)
                    vec.wait_ge(s_fin, f0 + 4)
                    nc.vector.tensor_scalar(small[:, 3, :], small[:, 2, :], -1.0, -1.0, ALU.mult, ALU.add)\
                      .then_inc(s_fin, 1)
                    vec.wait_ge(s_fin, f0 + 5)
                    nc.vector.reciprocal(small[:, 5, :], small[:, 3, :]).then_inc(s_fin, 1)
                    vec.wait_ge(s_fin, f0 + 6)
                    vec.wait_ge(s_q, XT * CPB * (b + 1))

                    def rest_of_q(k, t):
                        h = XT * ((2 * b + 1) * CPB + k) + t
                        vec.wait_ge(s_hi, h + 1)
                        nc.vector.scalar_tensor_tensor(lo(h), WW[:, t, k * N:(k + 1) * N], small[:, 5, t:t + 1],
                                                       f32(hi(h)), ALU.mult, ALU.subtract).then_inc(s_lo, 1)

                    def add_out(k, m):
                        u = (2 * b + 1) * CPB + k
                        vec.wait_ge(s_xl[u % 2], 16 * (u // 2 + 1))
                        vec.wait_ge(s_acc, XT * u + m + 1)
                        o = XC[:, u % 2, m, :]
                        nc.vector.tensor_tensor(o, o, p_w[:, m, :], ALU.add).then_inc(s_ev, 1)

                    for k in range(CPB):
                        for t in range(NR - 1):
                            rest_of_q(k, t)
                        if k:
                            for m in range(XT):
                                add_out(k - 1, m)
                        for t in range(NR - 1, XT):
                            rest_of_q(k, t)
                    for m in range(XT):
                        add_out(CPB - 1, m)


def kernel(**inputs):
    import numpy as np
    import concourse.bacc as bacc
    from concourse.bass_utils import run_bass_kernel_spmd

    a = {n.replace("L0_conv_", "").replace("L1_conv_", "l1_"): np.asarray(v) for n, v in inputs.items()}
    C, DI = 768, 1536
    XT, K = C // P, DI // P
    NH = a["l1_temp"].shape[0]

    def col(v):
        return v.reshape(K, P).T

    head = np.arange(C) // (C // NH)
    pick = np.zeros((P, 2, P), np.float32)
    pick[:64, 0] = pick[64:, 1] = 1.0 / (32 * DI)
    arrays = {
        "x": a["x"],
        "win": a["in_proj_w"].reshape(K, P, P, XT).transpose(0, 2, 3, 1),
        "wout": a["out_proj_w"].T.reshape(K, P, P, XT).transpose(1, 0, 3, 2).reshape(P, K, C),
        "xpw": a["x_proj_w"].T.reshape(K, P, -1).transpose(1, 0, 2),
        "dtw": a["dt_w"][0].T,
        "cw": a["conv_w"].reshape(K, P, 9).transpose(1, 0, 2),
        "cols": np.stack([col(a["conv_b"]), col(a["dt_b"][0]), col(a["D_param"][0]), col(a["ln_g"]),
                          col(a["ln_b"])], axis=1),
        "alog": a["A_log"][0].reshape(K, P, -1).transpose(1, 0, 2).reshape(P, -1),
        "wqkv": a["l1_W_qkv"].T.reshape(P, XT, C),
        "wo2": a["l1_W_out"].T.reshape(XT, P, P, XT).transpose(1, 0, 3, 2).reshape(P, XT, C),
        "temp": a["l1_temp"][head, 0].reshape(XT, P).T,
        "quad_d": np.kron(np.eye(P // 4), np.full((4, 4), 0.25)).astype(np.float32),
        "pick_d": pick,
        "sel_d": (head.reshape(XT, P).T[:, :, None] == np.arange(NH)).astype(np.float32),
        "selb_d": (np.arange(NH)[:, None] == head).astype(np.float32),
        "ident_d": np.eye(P, dtype=np.float32),
    }
    arrays = {"in_" + n: np.ascontiguousarray(v) for n, v in arrays.items()}
    nc = bacc.Bacc("TRN2", target_bir_lowering=False, num_devices=1)
    args = [nc.dram_tensor(n, v.shape, mybir.dt.from_np(v.dtype), kind="ExternalInput").ap()
            for n, v in arrays.items()]
    out = nc.dram_tensor("out", a["x"].shape, F32, kind="ExternalOutput").ap()
    build(nc, *args, out)
    r = run_bass_kernel_spmd(nc, [arrays], core_ids=[0])
    return r.results[0]["out"]
```
